# Optimizing a Trainium2 kernel written in Bass

```python
import numpy as np
import jax
import jax.numpy as jnp

def _softmax(x, axis=-1):
    return jax.nn.softmax(x, axis=axis)

def _gelu(x):
    return jax.nn.gelu(x, approximate=True)

def _silu(x):
    return jax.nn.silu(x)

def _sigmoid(x):
    return jax.nn.sigmoid(x)

def _layernorm(x, axis=-1, eps=1e-05):
    m = jnp.mean(x, axis=axis, keepdims=True)
    v = jnp.var(x, axis=axis, keepdims=True)
    return (x - m) / jnp.sqrt(v + eps)

def _scatter_add(tgt, idx, src, axis=0):
    return tgt.at[idx].add(src)

def _segment_sum(src, seg, n):
    return jax.ops.segment_sum(src, seg, n)
kernel_name = 'mk_xattn_seq_d2_seqx_r8_03f780'

def setup_inputs(seed: int=0):
    np.random.seed(seed)
    _w = jnp.asarray

    def _rec_inputs():
        import jax
        import jax.numpy as jnp
        _rk = jax.random.key(seed)
        x = -0.0005146 + 1 * jax.random.normal(jax.random.fold_in(_rk, 1), (64, 64, 256), jnp.float32)
        _lenS = 64 - jax.random.randint(jax.random.fold_in(_rk, 7), (64,), 0, max(1, 64 // 4) + 1, jnp.int32)
        _lenS2 = 64 - jax.random.randint(jax.random.fold_in(_rk, 8), (64,), 0, max(1, 64 // 4) + 1, jnp.int32)
        _ctx_2048P = jax.random.normal(jax.random.fold_in(_rk, 11), (64, 16, 256), jnp.float32)
        _ctx_2048c = jax.random.dirichlet(jax.random.fold_in(_rk, 511), 0.3 * jnp.ones((16,), jnp.float32), (64, 64))
        _ctx_2048t = jnp.einsum('bsk,bkd->bsd', _ctx_2048c, _ctx_2048P)
        _ctx_2048t = _ctx_2048t * jax.lax.rsqrt(jnp.mean(jnp.square(_ctx_2048t)) + 1e-12) * 0.953939
        ctx_2048 = -0.000392918 + 0.999932 * (_ctx_2048t + 0.3 * jax.random.normal(jax.random.fold_in(_rk, 611), (64, 64, 256), jnp.float32))
        _validS = jnp.arange(64)[None, :] < _lenS[:, None]
        _validS2 = jnp.arange(64)[None, :] < _lenS2[:, None]
        _causal = jnp.tril(jnp.ones((64, 64), dtype=bool))
        mask_BxS2_ik0 = jnp.where(jnp.broadcast_to(_validS2[:, :], (64, 64)), 0, 1).astype(jnp.int32)
        return (x, ctx_2048, mask_BxS2_ik0)
    x, ctx_2048, mask_BxS2_ik0 = _rec_inputs()

    def _L0_xattn_setup():
        import jax, jax.numpy as jnp
        import numpy as np
        B, P, K, H, NH = (4, 256, 32, 256, 16)
        DH = H // NH
        EPS = 1e-06

        def rmsnorm(x, w):
            var = jnp.mean(jnp.square(x), axis=-1, keepdims=True)
            return x * jax.lax.rsqrt(var + EPS) * w
        key = jax.random.key(seed)
        ks = jax.random.split(key, 12)
        s = 0.02
        return {'x': jax.random.normal(ks[0], (B, P, H), jnp.float32), 'latents': jax.random.normal(ks[1], (B, K, H), jnp.float32), 'attention_mask': jax.random.randint(ks[2], (B, P), 0, 2, jnp.int32), 'q_w': s * jax.random.normal(ks[3], (H, H), jnp.float32), 'q_b': jnp.zeros((H,), jnp.float32), 'kv_w': s * jax.random.normal(ks[4], (H, 2 * H), jnp.float32), 'kv_b': jnp.zeros((2 * H,), jnp.float32), 'out_w': s * jax.random.normal(ks[5], (H, H), jnp.float32), 'out_b': jnp.zeros((H,), jnp.float32), 'postnorm_w': jnp.ones((H,), jnp.float32), 'mlp_w1': s * jax.random.normal(ks[6], (H, 4 * H), jnp.float32), 'mlp_b1': jnp.zeros((4 * H,), jnp.float32), 'mlp_w2': s * jax.random.normal(ks[7], (4 * H, H), jnp.float32), 'mlp_b2': jnp.zeros((H,), jnp.float32)}
    _L0_xattn_all = _L0_xattn_setup()
    _L0_xattn_in = {k: v for k, v in _L0_xattn_all.items() if k in ('q_w', 'q_b', 'kv_w', 'kv_b', 'out_w', 'out_b', 'postnorm_w', 'mlp_w1', 'mlp_b1', 'mlp_w2', 'mlp_b2')}
    del _L0_xattn_all

    def _L1_xattn_setup():
        import jax, jax.numpy as jnp
        import numpy as np
        E, H, L, B = (256, 32, 128, 4)
        S = E // H
        DM, DD = (32, 64)

        def _ln(x, w, b, eps=1e-05):
            m = x.mean(-1, keepdims=True)
            v = ((x - m) ** 2).mean(-1, keepdims=True)
            return (x - m) / jnp.sqrt(v + eps) * w + b

        def _block(x, state, ln1_w, ln1_b, ln2_w, ln2_b, maa_x, maa_w1, maa_w2, maa_stack, time_decay, td_w1, td_w2, u, Wr, Wk, Wv, Wg, Wo, gn_w, gn_b, ffn_maa_k, ffn_maa_r, Wfk, Wfr, Wfv):
            b, l, e = x.shape
            h = u.shape[0]
            s_ = e // h
            xa = _ln(x, ln1_w, ln1_b)
            sx = jnp.concatenate([state[:, 1:2] - xa[:, :1], xa[:, :-1] - xa[:, 1:]], axis=1)
            xxx = jnp.tanh((xa + sx * maa_x) @ maa_w1).reshape(b, l, 5, DM)
            xxx = jnp.einsum('blfd,fde->blfe', xxx, maa_w2)
            xm = xa[:, :, None] + sx[:, :, None] * (maa_stack + xxx)
            xk, xw, xv, xr, xg = (xm[:, :, j] for j in range(5))
            w = jnp.exp(-jnp.exp(time_decay + jnp.tanh(xw @ td_w1) @ td_w2)).reshape(b, l, h, s_)
            r = (xr @ Wr.T).reshape(b, l, h, s_)
            k = (xk @ Wk.T).reshape(b, l, h, s_)
            v = (xv @ Wv.T).reshape(b, l, h, s_)
            g = jax.nn.silu(xg @ Wg.T)
            s0 = state[:, 2:2 + s_].reshape(b, h, s_, s_)

            def step(s, rkvw):
                r_t, k_t, v_t, w_t = rkvw
                a = k_t[..., :, None] * v_t[..., None, :]
                out = jnp.einsum('bhi,bhij->bhj', r_t, u * a + s)
                s = a + w_t[..., :, None] * s
                return (s, out)
            rkvw = tuple((jnp.moveaxis(t, 1, 0) for t in (r, k, v, w)))
            _, out = jax.lax.scan(step, s0, rkvw)
            out = jnp.moveaxis(out, 0, 1).reshape(b, l, e)
            og = out.reshape(b, l, h, s_)
            m = og.mean(-1, keepdims=True)
            va = ((og - m) ** 2).mean(-1, keepdims=True)
            og = ((og - m) / jnp.sqrt(va + 1e-05)).reshape(b, l, e) * gn_w + gn_b
            x1 = x + og * g @ Wo.T
            xc = _ln(x1, ln2_w, ln2_b)
            sx2 = jnp.concatenate([state[:, 0:1] - xc[:, :1], xc[:, :-1] - xc[:, 1:]], axis=1)
            xk2 = xc + sx2 * ffn_maa_k
            xr2 = xc + sx2 * ffn_maa_r
            rr = jax.nn.sigmoid(xr2 @ Wfr.T)
            kk = jnp.square(jax.nn.relu(xk2 @ Wfk.T))
            return x1 + rr * (kk @ Wfv.T)
        key = jax.random.key(seed)
        ks = jax.random.split(key, 24)
        sc = 0.02
        d = {'x': jax.random.normal(ks[0], (B, L, E), jnp.float32), 'state': jax.random.normal(ks[1], (B, 2 + S, E), jnp.float32) * 0.1, 'ln1_w': jnp.ones((E,), jnp.float32), 'ln1_b': jnp.zeros((E,), jnp.float32), 'ln2_w': jnp.ones((E,), jnp.float32), 'ln2_b': jnp.zeros((E,), jnp.float32), 'maa_x': jax.random.normal(ks[2], (E,), jnp.float32) * 0.1, 'maa_w1': jax.random.normal(ks[3], (E, 5 * DM), jnp.float32) * sc, 'maa_w2': jax.random.normal(ks[4], (5, DM, E), jnp.float32) * sc, 'maa_stack': jax.random.normal(ks[5], (1, 5, E), jnp.float32) * 0.1, 'time_decay': jax.random.normal(ks[6], (E,), jnp.float32) * 0.5, 'td_w1': jax.random.normal(ks[7], (E, DD), jnp.float32) * sc, 'td_w2': jax.random.normal(ks[8], (DD, E), jnp.float32) * sc, 'u': jax.random.normal(ks[9], (H, S, 1), jnp.float32) * 0.1, 'Wr': jax.random.normal(ks[10], (E, E), jnp.float32) * sc, 'Wk': jax.random.normal(ks[11], (E, E), jnp.float32) * sc, 'Wv': jax.random.normal(ks[12], (E, E), jnp.float32) * sc, 'Wg': jax.random.normal(ks[13], (E, E), jnp.float32) * sc, 'Wo': jax.random.normal(ks[14], (E, E), jnp.float32) * sc, 'gn_w': jnp.ones((E,), jnp.float32), 'gn_b': jnp.zeros((E,), jnp.float32), 'ffn_maa_k': jax.random.normal(ks[15], (E,), jnp.float32) * 0.1, 'ffn_maa_r': jax.random.normal(ks[16], (E,), jnp.float32) * 0.1, 'Wfk': jax.random.normal(ks[17], (E, E), jnp.float32) * sc, 'Wfr': jax.random.normal(ks[18], (E, E), jnp.float32) * sc, 'Wfv': jax.random.normal(ks[19], (E, E), jnp.float32) * sc}
        return d
    _L1_xattn_all = _L1_xattn_setup()
    _L1_xattn_in = {k: v for k, v in _L1_xattn_all.items() if k in ('ln1_w', 'ln1_b', 'ln2_w', 'ln2_b', 'maa_x', 'maa_w1', 'maa_w2', 'maa_stack', 'time_decay', 'td_w1', 'td_w2', 'u', 'Wr', 'Wk', 'Wv', 'Wg', 'Wo', 'gn_w', 'gn_b', 'ffn_maa_k', 'ffn_maa_r', 'Wfk', 'Wfr', 'Wfv')}
    del _L1_xattn_all
    return {'x': x, 'ctx_2048': ctx_2048, 'mask_BxS2_ik0': mask_BxS2_ik0, 'L0_xattn_q_w': _L0_xattn_in['q_w'], 'L0_xattn_q_b': _L0_xattn_in['q_b'], 'L0_xattn_kv_w': _L0_xattn_in['kv_w'], 'L0_xattn_kv_b': _L0_xattn_in['kv_b'], 'L0_xattn_out_w': _L0_xattn_in['out_w'], 'L0_xattn_out_b': _L0_xattn_in['out_b'], 'L0_xattn_postnorm_w': _L0_xattn_in['postnorm_w'], 'L0_xattn_mlp_w1': _L0_xattn_in['mlp_w1'], 'L0_xattn_mlp_b1': _L0_xattn_in['mlp_b1'], 'L0_xattn_mlp_w2': _L0_xattn_in['mlp_w2'], 'L0_xattn_mlp_b2': _L0_xattn_in['mlp_b2'], 'L1_xattn_ln1_w': _L1_xattn_in['ln1_w'], 'L1_xattn_ln1_b': _L1_xattn_in['ln1_b'], 'L1_xattn_ln2_w': _L1_xattn_in['ln2_w'], 'L1_xattn_ln2_b': _L1_xattn_in['ln2_b'], 'L1_xattn_maa_x': _L1_xattn_in['maa_x'], 'L1_xattn_maa_w1': _L1_xattn_in['maa_w1'], 'L1_xattn_maa_w2': _L1_xattn_in['maa_w2'], 'L1_xattn_maa_stack': _L1_xattn_in['maa_stack'], 'L1_xattn_time_decay': _L1_xattn_in['time_decay'], 'L1_xattn_td_w1': _L1_xattn_in['td_w1'], 'L1_xattn_td_w2': _L1_xattn_in['td_w2'], 'L1_xattn_u': _L1_xattn_in['u'], 'L1_xattn_Wr': _L1_xattn_in['Wr'], 'L1_xattn_Wk': _L1_xattn_in['Wk'], 'L1_xattn_Wv': _L1_xattn_in['Wv'], 'L1_xattn_Wg': _L1_xattn_in['Wg'], 'L1_xattn_Wo': _L1_xattn_in['Wo'], 'L1_xattn_gn_w': _L1_xattn_in['gn_w'], 'L1_xattn_gn_b': _L1_xattn_in['gn_b'], 'L1_xattn_ffn_maa_k': _L1_xattn_in['ffn_maa_k'], 'L1_xattn_ffn_maa_r': _L1_xattn_in['ffn_maa_r'], 'L1_xattn_Wfk': _L1_xattn_in['Wfk'], 'L1_xattn_Wfr': _L1_xattn_in['Wfr'], 'L1_xattn_Wfv': _L1_xattn_in['Wfv']}

def reference(x, ctx_2048, mask_BxS2_ik0, L0_xattn_q_w, L0_xattn_q_b, L0_xattn_kv_w, L0_xattn_kv_b, L0_xattn_out_w, L0_xattn_out_b, L0_xattn_postnorm_w, L0_xattn_mlp_w1, L0_xattn_mlp_b1, L0_xattn_mlp_w2, L0_xattn_mlp_b2, L1_xattn_ln1_w, L1_xattn_ln1_b, L1_xattn_ln2_w, L1_xattn_ln2_b, L1_xattn_maa_x, L1_xattn_maa_w1, L1_xattn_maa_w2, L1_xattn_maa_stack, L1_xattn_time_decay, L1_xattn_td_w1, L1_xattn_td_w2, L1_xattn_u, L1_xattn_Wr, L1_xattn_Wk, L1_xattn_Wv, L1_xattn_Wg, L1_xattn_Wo, L1_xattn_gn_w, L1_xattn_gn_b, L1_xattn_ffn_maa_k, L1_xattn_ffn_maa_r, L1_xattn_Wfk, L1_xattn_Wfr, L1_xattn_Wfv):
    import jax
    import jax.numpy as jnp

    def _L0_xattn_ref(x, latents, attention_mask, q_w, q_b, kv_w, kv_b, out_w, out_b, postnorm_w, mlp_w1, mlp_b1, mlp_w2, mlp_b2):
        import jax, jax.numpy as jnp
        import numpy as np
        B, P, K, H, NH = (4, 256, 32, 256, 16)
        DH = H // NH
        EPS = 1e-06

        def rmsnorm(x, w):
            var = jnp.mean(jnp.square(x), axis=-1, keepdims=True)
            return x * jax.lax.rsqrt(var + EPS) * w
        b, p, _ = x.shape
        k_len = latents.shape[1]
        residual = latents
        h = jnp.concatenate([x, latents], axis=1)
        q = (latents @ q_w + q_b).reshape(b, k_len, NH, DH)
        kv = (h @ kv_w + kv_b).reshape(b, p + k_len, NH, DH, 2)
        kmat, v = (kv[..., 0], kv[..., 1])
        attn = jnp.einsum('bkhd,bnhd->bhkn', q, kmat) / DH
        full_mask = jnp.concatenate([attention_mask.astype(bool), jnp.ones((b, k_len), bool)], axis=-1)
        attn = jnp.where(full_mask[:, None, None, :], attn, -jnp.inf)
        attn = jax.nn.softmax(attn.astype(jnp.float32), axis=-1).astype(q.dtype)
        attn_out = jnp.einsum('bhkn,bnhd->bkhd', attn, v).reshape(b, k_len, H)
        attn_out = attn_out @ out_w + out_b + residual
        out = rmsnorm(attn_out, postnorm_w)
        out = jax.nn.gelu(out @ mlp_w1 + mlp_b1) @ mlp_w2 + mlp_b2
        return out + residual

    def _L1_xattn_ref(x, state, ln1_w, ln1_b, ln2_w, ln2_b, maa_x, maa_w1, maa_w2, maa_stack, time_decay, td_w1, td_w2, u, Wr, Wk, Wv, Wg, Wo, gn_w, gn_b, ffn_maa_k, ffn_maa_r, Wfk, Wfr, Wfv):
        import jax, jax.numpy as jnp
        import numpy as np
        E, H, L, B = (256, 32, 128, 4)
        S = E // H
        DM, DD = (32, 64)

        def _ln(x, w, b, eps=1e-05):
            m = x.mean(-1, keepdims=True)
            v = ((x - m) ** 2).mean(-1, keepdims=True)
            return (x - m) / jnp.sqrt(v + eps) * w + b

        def _block(x, state, ln1_w, ln1_b, ln2_w, ln2_b, maa_x, maa_w1, maa_w2, maa_stack, time_decay, td_w1, td_w2, u, Wr, Wk, Wv, Wg, Wo, gn_w, gn_b, ffn_maa_k, ffn_maa_r, Wfk, Wfr, Wfv):
            b, l, e = x.shape
            h = u.shape[0]
            s_ = e // h
            xa = _ln(x, ln1_w, ln1_b)
            sx = jnp.concatenate([state[:, 1:2] - xa[:, :1], xa[:, :-1] - xa[:, 1:]], axis=1)
            xxx = jnp.tanh((xa + sx * maa_x) @ maa_w1).reshape(b, l, 5, DM)
            xxx = jnp.einsum('blfd,fde->blfe', xxx, maa_w2)
            xm = xa[:, :, None] + sx[:, :, None] * (maa_stack + xxx)
            xk, xw, xv, xr, xg = (xm[:, :, j] for j in range(5))
            w = jnp.exp(-jnp.exp(time_decay + jnp.tanh(xw @ td_w1) @ td_w2)).reshape(b, l, h, s_)
            r = (xr @ Wr.T).reshape(b, l, h, s_)
            k = (xk @ Wk.T).reshape(b, l, h, s_)
            v = (xv @ Wv.T).reshape(b, l, h, s_)
            g = jax.nn.silu(xg @ Wg.T)
            s0 = state[:, 2:2 + s_].reshape(b, h, s_, s_)

            def step(s, rkvw):
                r_t, k_t, v_t, w_t = rkvw
                a = k_t[..., :, None] * v_t[..., None, :]
                out = jnp.einsum('bhi,bhij->bhj', r_t, u * a + s)
                s = a + w_t[..., :, None] * s
                return (s, out)
            rkvw = tuple((jnp.moveaxis(t, 1, 0) for t in (r, k, v, w)))
            _, out = jax.lax.scan(step, s0, rkvw)
            out = jnp.moveaxis(out, 0, 1).reshape(b, l, e)
            og = out.reshape(b, l, h, s_)
            m = og.mean(-1, keepdims=True)
            va = ((og - m) ** 2).mean(-1, keepdims=True)
            og = ((og - m) / jnp.sqrt(va + 1e-05)).reshape(b, l, e) * gn_w + gn_b
            x1 = x + og * g @ Wo.T
            xc = _ln(x1, ln2_w, ln2_b)
            sx2 = jnp.concatenate([state[:, 0:1] - xc[:, :1], xc[:, :-1] - xc[:, 1:]], axis=1)
            xk2 = xc + sx2 * ffn_maa_k
            xr2 = xc + sx2 * ffn_maa_r
            rr = jax.nn.sigmoid(xr2 @ Wfr.T)
            kk = jnp.square(jax.nn.relu(xk2 @ Wfk.T))
            return x1 + rr * (kk @ Wfv.T)
        return _block(x, state, ln1_w, ln1_b, ln2_w, ln2_b, maa_x, maa_w1, maa_w2, maa_stack, time_decay, td_w1, td_w2, u, Wr, Wk, Wv, Wg, Wo, gn_w, gn_b, ffn_maa_k, ffn_maa_r, Wfk, Wfr, Wfv)
    x = _L0_xattn_ref(ctx_2048, x, mask_BxS2_ik0, L0_xattn_q_w, L0_xattn_q_b, L0_xattn_kv_w, L0_xattn_kv_b, L0_xattn_out_w, L0_xattn_out_b, L0_xattn_postnorm_w, L0_xattn_mlp_w1, L0_xattn_mlp_b1, L0_xattn_mlp_w2, L0_xattn_mlp_b2)
    x = _L1_xattn_ref(x, ctx_2048, L1_xattn_ln1_w, L1_xattn_ln1_b, L1_xattn_ln2_w, L1_xattn_ln2_b, L1_xattn_maa_x, L1_xattn_maa_w1, L1_xattn_maa_w2, L1_xattn_maa_stack, L1_xattn_time_decay, L1_xattn_td_w1, L1_xattn_td_w2, L1_xattn_u, L1_xattn_Wr, L1_xattn_Wk, L1_xattn_Wv, L1_xattn_Wg, L1_xattn_Wo, L1_xattn_gn_w, L1_xattn_gn_b, L1_xattn_ffn_maa_k, L1_xattn_ffn_maa_r, L1_xattn_Wfk, L1_xattn_Wfr, L1_xattn_Wfv)
    return x

_drawn_inputs = setup_inputs


def setup_inputs(seed=0):
    import zlib

    import numpy as np

    out = dict(_drawn_inputs(seed))
    spreads = {'L0_xattn_q_b': (0.0, 0.8),
     'L0_xattn_kv_b': (0.0, 0.8),
     'L0_xattn_out_b': (0.0, 2.0),
     'L0_xattn_postnorm_w': (1.0, 0.6),
     'L0_xattn_mlp_b1': (0.0, 0.1),
     'L0_xattn_mlp_b2': (0.0, 0.1),
     'L1_xattn_ln1_w': (1.0, 0.6),
     'L1_xattn_ln1_b': (0.0, 0.575),
     'L1_xattn_ln2_w': (1.0, 0.6),
     'L1_xattn_ln2_b': (0.0, 0.8),
     'L1_xattn_gn_w': (1.0, 0.6),
     'L1_xattn_gn_b': (0.0, 0.8)}
    factors = {'ctx_2048': 4.055,
     'L0_xattn_q_w': 8.0,
     'L0_xattn_kv_w': 8.0,
     'L0_xattn_out_w': 8.0,
     'L1_xattn_maa_x': 8.0,
     'L1_xattn_maa_w1': 7.909,
     'L1_xattn_maa_w2': 7.814,
     'L1_xattn_maa_stack': 2.878,
     'L1_xattn_time_decay': 2.8,
     'L1_xattn_td_w1': 8.0,
     'L1_xattn_td_w2': 8.0,
     'L1_xattn_u': 5.973,
     'L1_xattn_ffn_maa_k': 8.0,
     'L1_xattn_ffn_maa_r': 8.0,
     'L1_xattn_Wfk': 2.818,
     'L1_xattn_Wfr': 8.0}
    for name, (base, spread) in spreads.items():
        noise = np.random.default_rng([zlib.crc32(name.encode()), seed]).standard_normal(out[name].shape)
        drawn = base * np.exp(spread * noise) if base else spread * noise
        out[name] = jnp.asarray(drawn.astype(out[name].dtype))
    for name, factor in factors.items():
        out[name] = (out[name] * factor).astype(out[name].dtype)
    return out
```

```python
import concourse.bass as bass
from concourse import mybir
from contextlib import ExitStack

B, S, C = 64, 64, 256
P = 128
HALVES = C // P
GB = 8
GROUPS = B // GB
T = GB * S
KEYS = 2 * S
HEADS, DH = 16, 16
PAIRS = P // (2 * DH)
UNITS = (GB // 2) * PAIRS
F = 4 * C
FM = F // P
RH = 8
DM, DD = 32, 64
MIX = 5
ORDER = (1, 0, 2, 3, 4)
FIRST = 0
NEG = -1e30

W_COLS = {}
at = 0
for _name, _n in (("q", C), ("k", C), ("v", C), ("o", C), ("w1", F), ("maa1", MIX * DM), ("td1", DD),
                  ("Wr", C), ("Wk", C), ("Wv", C), ("Wg", C), ("Wo", C), ("Wfk", C), ("Wfr", C), ("Wfv", C)):
    W_COLS[_name] = (at, at + _n)
    at += _n
W_TOTAL = at
W_PARTS = (("q", "v"), ("o", "w1"), ("maa1", "Wfv"))

V_COLS = {}
at = 0
for _name, _n in (("q_b", 2), ("k_b", 2), ("v_b", 2), ("o_b", 2), ("pn", 2), ("b1", FM), ("b2", 2), ("ln1_w", 2), ("ln1_b", 2),
                  ("ln2_w", 2), ("ln2_b", 2), ("maa_x", 2), ("maa", 2 * MIX), ("td", 2), ("gn_w", 2), ("gn_b", 2),
                  ("fk", 2), ("fr", 2), ("u", 2), ("even", 1), ("odd", 1), ("even16", 1), ("odd16", 1), ("eps6", 1), ("eps5", 1)):
    V_COLS[_name] = at
    at += _n
V_TOTAL = at

M_NAMES = ["ident", "mean256", "mean8", "center8", "same_head"] + [f"spread{j}" for j in range(RH)] + [f"gather{j}" for j in range(RH)]
M_COL = {n: i for i, n in enumerate(M_NAMES)}


def slots(names, banks):
    return {n: (i % banks, i // banks) for i, n in enumerate(names)}, [len(names[b::banks]) for b in range(banks)]


A_NAMES = ([("q", m) for m in range(2)] + [("k", m, n) for m in range(2) for n in range(2)] + [("v", n) for n in range(4)]
           + [("s", u) for u in range(UNITS)] + [("o", m) for m in range(2)] + [("rms",)] + [("w1", m) for m in range(FM)])
A_SLOT, A_USES = slots(A_NAMES, 2)
R_NAMES = ([("mean", 0), ("var", 0), ("maa", 0), ("maa", 1), ("x", 0, 0), ("x", 0, 1), ("x", 1, 0), ("x", 1, 1), ("td1",),
            ("x", 2, 0), ("x", 2, 1), ("td2", 0), ("td2", 1), ("K", 0), ("K", 1), ("x", 3, 0), ("x", 3, 1), ("V", 0), ("V", 1),
            ("x", 4, 0), ("x", 4, 1), ("R", 0), ("R", 1), ("G", 0), ("G", 1)]
           + [("spread", 0, j) for j in range(RH)] + [("coef", 0)]
           + [("spread", 1, j) for j in range(4)] + [("gvar", 0)] + [("spread", 1, j) for j in range(4, RH)] + [("coef", 1)]
           + [("gvar", 1), ("O", 0), ("O", 1), ("mean", 1), ("var", 1)]
           + [("fk", 0), ("fk", 1), ("fr", 0), ("fr", 1), ("fv", 0), ("fv", 1)])
R_SLOT, R_USES = slots(R_NAMES, 3)

TURN = [("A", "qk"), ("R", "mean0"), ("A", "v"), ("R", "var0"), ("A", "u0"), ("R", "maa"), ("A", "u1"), ("R", "x0"),
        ("A", "u2"), ("R", "x1"), ("A", "u3"), ("R", "x2"), ("A", "u4"), ("R", "x3"), ("A", "u5"), ("R", "x4"),
        ("A", "u6"), ("R", "G"), ("R", "s00"), ("A", "u7"), ("R", "s01"), ("A", "u8"), ("R", "s02"), ("A", "u9"), ("R", "s03"),
        ("A", "u10"), ("R", "s10"), ("A", "u11"), ("R", "s11"), ("A", "u12"), ("R", "s12"), ("A", "u13"), ("R", "s13"),
        ("A", "u14"), ("A", "u15"), ("R", "gn"), ("A", "u16"), ("A", "u17"), ("A", "u18"), ("A", "o"), ("R", "O"), ("A", "rms"), ("R", "mean1"),
        ("A", "mlp0"), ("R", "var1"), ("A", "mlp1"), ("R", "shift"), ("A", "x1"), ("R", "ffn")]


def build(nc, hT, xT, maskT, stT, s0T, W, W2, MAA2, TD2, VEC, MATS, out):
    fp32, bf16, i32 = mybir.dt.float32, mybir.dt.bfloat16, mybir.dt.int32
    ALU, ACT, AX = mybir.AluOpType, mybir.ActivationFunctionType, mybir.AxisListType

    with ExitStack() as ctx:
        def sb(name, shape, dt=fp32):
            return ctx.enter_context(nc.sbuf_tensor(name, shape, dt))

        class Event:
            def __init__(self, name, per_group):
                self.sem, self.n = ctx.enter_context(nc.semaphore(name)), per_group

        def count(event, g, k):
            value = g * event.n + k
            return max(value, 0) if isinstance(value, int) else value

        w_sb = sb("w_sb", [P, HALVES, W_TOTAL])
        w2_sb = sb("w2_sb", [P, FM, C])
        maa2_sb = sb("maa2_sb", [P, MIX, C])
        td2_sb = sb("td2_sb", [P, C])
        vec = sb("vec", [P, V_TOTAL])
        mats = sb("mats", [P, len(M_NAMES), P])
        bonus_w = sb("bonus_w", [P, HALVES, P])
        q_bias = sb("q_bias", [P, 2, HALVES])
        o_bias = sb("o_bias", [P, HALVES])
        ones_bf = sb("ones_bf", [P, P], bf16)

        def w(name, k, a=0, b=None):
            lo, hi = W_COLS[name]
            return w_sb[:, k, lo + a:(hi if b is None else lo + b)]

        def v(name, i=0):
            c = V_COLS[name] + i
            return vec[:, c:c + 1]

        def mat(name):
            return mats[:, M_COL[name], :]

        h_sb = sb("h_sb", [P, HALVES, GB, KEYS])
        xa_sb = sb("xa_sb", [P, HALVES, T])
        mask_i = sb("mask_i", [P, GB, S], i32)
        mask_b = sb("mask_b", [P, GB, S], bf16)
        qt = sb("qt", [P, HALVES, GB, 2, S])
        kt = sb("kt", [P, HALVES, GB, KEYS])
        vv = sb("vv", [P, GB, C])
        neg_max = sb("neg_max", [P, 2, 4])
        sums = sb("sums", [P, 2, 4])
        rsum = sb("rsum", [P, 2, 4])
        probs = sb("probs", [P, 3, 4, KEYS])
        probs_t = sb("probs_t", [P, 2, 4, P])
        o_even = sb("o_even", [P, 4, S])
        attn = sb("attn", [P, GB, HALVES, S])
        ysq = attn[:, :, :, :].rearrange("p b h s -> p (b h s)").rearrange("p (h t) -> p h t", h=HALVES)
        y = sb("y", [P, HALVES, T])
        a_ms = sb("a_ms", [P, T])
        hid = sb("hid", [P, 2, T])
        x1 = sb("x1", [P, HALVES, T])

        st_sb = sb("st_sb", [P, 2, HALVES, GB])
        s0_sb = sb("s0_sb", [P, HALVES, RH, GB])
        xc = sb("xc", [P, HALVES, T])
        og = xc
        sx = sb("sx", [P, HALVES, T])
        sq = sx
        r_ms = sb("r_ms", [P, T])
        xs = sb("xs", [P, HALVES, GB, S + 1])
        th = sb("th", [P, 2, T])
        tmp = sb("tmp", [P, 2, T])
        g_ms = tmp
        xm = sb("xm", [P, 2, HALVES, T])
        tw = sb("tw", [P, T])
        e1 = sb("e1", [P, 2, T])
        gt, gsq, tr = e1, e1, e1
        decay = sb("decay", [P, HALVES, GB, S])
        rr = sb("rr", [P, HALVES, T])
        kk = sb("kk", [P, HALVES, T])
        vr = sb("vr", [P, HALVES, T])
        act, relu = rr, kk
        gate = sb("gate", [P, HALVES, T])
        kv = sb("kv", [P, 4, GB, S])
        st = sb("st", [P, 2, T])
        rs = sb("rs", [P, 2, T])
        rk = sb("rk", [P, T])
        bonus = rk
        x2 = sb("x2", [P, HALVES, T])

        psum = [ctx.enter_context(nc.psum_tensor(f"bank{i}", [P, 512], fp32)) for i in range(8)]
        A_BANK, R_BANK = psum[0:2], psum[4:7]
        pt_ps, o_ps, red_ps = psum[2], psum[3], psum[7]

        def by_batch(ap):
            return ap.rearrange("p (b s) -> p b s", b=GB)

        def both(ap):
            return ap.unsqueeze(1).broadcast_to([P, HALVES, T])

        ld_vec, ld_mats, ld_w2, ld_small = (Event(n, 0) for n in ("vec_in", "mats_in", "w2_in", "small_in"))
        ld_w = [Event(f"weights_in{i}", 0) for i in range(3)]
        fills, folded, bias_sum = Event("fills", 0), Event("folded", 0), Event("bias_sum", 0)
        h_in, xa_in, mask_in, st_in, s0_in = (Event(n, 16) for n in ("h_in", "xa_in", "mask_in", "st_in", "s0_in"))
        out_done = Event("out_done", 16)
        a_full = [Event(f"a_full{i}", A_USES[i]) for i in range(2)]
        a_free = [Event(f"a_free{i}", A_USES[i]) for i in range(2)]
        r_full = [Event(f"r_full{i}", R_USES[i]) for i in range(3)]
        r_free = [Event(f"r_free{i}", R_USES[i]) for i in range(3)]
        pt_full, pt_free = Event("pt_full", UNITS + 1), Event("pt_free", UNITS + 1)
        o_full, o_free = Event("o_full", 5), Event("o_free", 5)
        red_full, red_free = Event("red_full", 2), Event("red_free", 2)
        mask_made = Event("mask_made", 1)
        max_made, rsum_made, norm_made = (Event(n, UNITS) for n in ("max_made", "rsum_made", "norm_made"))
        o_even_made = Event("o_even_made", 4)
        ysq_made, arstd_made, yn_made = Event("ysq_made", 1), Event("arstd_made", 1), Event("yn_made", 1)
        sq_made, rstd_made, xn_made = (Event(n, 2) for n in ("sq_made", "rstd_made", "xn_made"))
        xs_made, row_made, sx_made = Event("xs_made", 4), Event("row_made", 2), Event("sx_made", 2)
        z_made, xm_made = Event("z_made", 2), Event("xm_made", 2 * MIX)
        decay_made, gt_made = Event("decay_made", 2), Event("gt_made", 2)
        first_made, st_made, rs_made = Event("first_made", 8), Event("st_made", 2 * RH), Event("rs_made", 2 * RH)
        rk_made = Event("rk_made", 2)
        og_made, grstd_made, gn1_made, gn2_made, gn3_made = (Event(n, 2) for n in ("og_made", "grstd_made", "gn1_made", "gn2_made", "gn3_made"))
        shift_made, act_made, fin_made = Event("shift_made", 4), Event("act_made", 2), Event("fin_made", 2)

        def a_bank(*name):
            return A_BANK[A_SLOT[name][0]]

        def a_open(g, *name):
            b, use = A_SLOT[name]
            return a_free[b].sem, count(a_free[b], g, use)

        def a_ready(g, *name):
            b, use = A_SLOT[name]
            return a_full[b].sem, count(a_full[b], g, use + 1)

        def a_taken(g, *name):
            b, use = A_SLOT[name]
            return a_free[b].sem, count(a_free[b], g, use + 1)

        def a_filled(*name):
            return a_full[A_SLOT[name][0]].sem

        def a_read(*name):
            return a_free[A_SLOT[name][0]].sem

        def r_bank(*name):
            return R_BANK[R_SLOT[name][0]]

        def r_open(g, *name):
            b, use = R_SLOT[name]
            return r_free[b].sem, count(r_free[b], g, use)

        def r_ready(g, *name):
            b, use = R_SLOT[name]
            return r_full[b].sem, count(r_full[b], g, use + 1)

        def r_taken(g, *name):
            b, use = R_SLOT[name]
            return r_free[b].sem, count(r_free[b], g, use + 1)

        def r_filled(*name):
            return r_full[R_SLOT[name][0]].sem

        def r_read(*name):
            return r_free[R_SLOT[name][0]].sem

        def run(eng, attention, recurrent):
            def turn(i):
                for stream, piece in TURN:
                    if stream == "A":
                        attention(i, piece)
                    else:
                        recurrent(i - 1, piece)

            for stream, piece in TURN:
                if stream == "A":
                    attention(FIRST, piece)
            turn(1)
            with eng.Fori(2, GROUPS) as i:
                turn(i)
            for stream, piece in TURN:
                if stream == "R":
                    recurrent(GROUPS - 1, piece)

        block = ctx.enter_context(nc.Block())

        @block.sync
        def _(sp):
            def load_attention(g):
                b, use = A_SLOT[("v", 3)]
                sp.wait_ge(a_full[b].sem, count(a_full[b], g, use + 1 - a_full[b].n))
                sp.dma_start(h_sb[:, :, :, :], hT[g, :, :, :, :]).then_inc(h_in.sem, 16)
                sp.wait_ge(mask_made.sem, count(mask_made, g, 0))
                sp.dma_start(mask_i[:, :, :].rearrange("p b s -> p (b s)"), maskT[g, :].partition_broadcast(P)).then_inc(mask_in.sem, 16)

            def load_residual(g):
                sp.wait_ge(pt_free.sem, count(pt_free, g - 1, UNITS + 1))
                sp.wait_ge(o_free.sem, count(o_free, g - 1, 5))
                sp.dma_start(xa_sb[:, :, :], xT[g, :, :, :]).then_inc(xa_in.sem, 16)

            def load_state(g):
                sp.wait_ge(row_made.sem, count(row_made, g, 0))
                sp.dma_start(st_sb[:, :, :, :], stT[g, :, :, :, :]).then_inc(st_in.sem, 16)
                sp.wait_ge(first_made.sem, count(first_made, g, 0))
                sp.dma_start(s0_sb[:, :, :, :], s0T[g, :, :, :, :]).then_inc(s0_in.sem, 16)

            def store(g):
                sp.wait_ge(fin_made.sem, count(fin_made, g, 2))
                sp.dma_start(out[g, :, :, :], x2[:, :, :]).then_inc(out_done.sem, 16)

            def load_weights(n):
                lo, hi = W_COLS[W_PARTS[n][0]][0], W_COLS[W_PARTS[n][1]][1]
                sp.dma_start(w_sb[:, :, lo:hi], W[:, :, lo:hi]).then_inc(ld_w[n].sem, 16)

            sp.dma_start(vec[:, :], VEC[:, :]).then_inc(ld_vec.sem, 16)
            load_weights(0)
            load_attention(0)
            sp.dma_start(mats[:, :, :], MATS[:, :, :]).then_inc(ld_mats.sem, 16)
            load_weights(1)
            load_residual(0)
            sp.dma_start(w2_sb[:, :, :], W2[:, :, :]).then_inc(ld_w2.sem, 16)
            load_weights(2)
            sp.dma_start(maa2_sb[:, :, :], MAA2[:, :, :]).then_inc(ld_small.sem, 16)
            sp.dma_start(td2_sb[:, :], TD2[:, :]).then_inc(ld_small.sem, 16)
            load_state(0)
            load_attention(1)
            load_residual(1)

            def turn(i):
                load_attention(i + 1)
                load_state(i)
                load_residual(i + 1)
                store(i - 1)

            turn(1)
            with sp.Fori(2, GROUPS - 1) as i:
                turn(i)
            load_state(GROUPS - 1)
            store(GROUPS - 2)
            store(GROUPS - 1)
            sp.wait_ge(out_done.sem, 16 * GROUPS)

        @block.tensor
        def _(pe):
            mm = nc.tensor.matmul

            def project(bank, name, m, rhs, width=P):
                mm(bank[0:width, :], w(name, 0, m * P, m * P + width), rhs[0], start=True, stop=False)
                return mm(bank[0:width, :], w(name, 1, m * P, m * P + width), rhs[1], start=False, stop=True)

            def average(bank, src):
                mm(bank[:, :], mat("mean256"), src[:, 0, :], start=True, stop=False)
                return mm(bank[:, :], mat("mean256"), src[:, 1, :], start=False, stop=True)

            def scores(g, u):
                bp, r = unit(u)
                bank = a_bank("s", u)
                pe.wait_ge(*a_open(g, "s", u))
                rows = slice(32 * r, 32 * r + 32)
                for n in range(4):
                    b, h = 2 * bp + n // 2, n % 2
                    mm(bank[:, n * P:(n + 1) * P], qt[rows, h, b, :, :].rearrange("p e s -> p (e s)"), kt[rows, h, b, :],
                       start=(n == 0), stop=False, skip_group_check=True)
                row = slice(32 * r, 32 * r + 1)
                for n in range(4):
                    last = mm(bank[:, n * P:n * P + S], ones_bf[row, :], mask_b[row, 2 * bp + n // 2, :],
                              start=False, stop=True, skip_group_check=True)
                last.then_inc(a_filled("s", u), 1)

            def transpose(g, u):
                pe.wait_ge(norm_made.sem, count(norm_made, g, u + 1))
                pe.wait_ge(pt_free.sem, count(pt_free, g, u))
                for n in range(4):
                    last = nc.tensor.transpose(pt_ps[:, n * P:(n + 1) * P], probs[:, u % 3, n, :], mat("ident"))
                last.then_inc(pt_full.sem, 1)

            def values(g, u):
                bp, r = unit(u)
                pe.wait_ge(pt_free.sem, count(pt_free, g, u + 1))
                if r == 0:
                    pe.wait_ge(o_free.sem, count(o_free, g, bp))
                for n in range(4):
                    b, h = 2 * bp + n // 2, n % 2
                    last = mm(o_ps[32 * r:32 * r + 32, n * P:(n + 1) * P], vv[:, b, h * P + 32 * r:h * P + 32 * r + 32],
                              probs_t[:, u % 2, n, :], start=True, stop=True)
                if r == PAIRS - 1:
                    last.then_inc(o_full.sem, 1)

            def attention(g, piece):
                if piece == "qk":
                    if g is FIRST:
                        pe.wait_ge(ld_w[0].sem, 16)
                    pe.wait_ge(h_in.sem, count(h_in, g, 16))
                    for m in range(2):
                        bank = a_bank("q", m)
                        pe.wait_ge(*a_open(g, "q", m))
                        project(bank, "q", m, [h_sb[:, k, :, S:KEYS] for k in range(2)]).then_inc(a_filled("q", m), 1)
                    for m in range(2):
                        for n in range(2):
                            bank = a_bank("k", m, n)
                            pe.wait_ge(*a_open(g, "k", m, n))
                            project(bank, "k", m, [h_sb[:, k, 4 * n:4 * n + 4, :] for k in range(2)]).then_inc(a_filled("k", m, n), 1)
                elif piece == "v":
                    for n in range(4):
                        bank = a_bank("v", n)
                        pe.wait_ge(*a_open(g, "v", n))
                        for i in range(2):
                            for k in range(2):
                                last = mm(bank[:, i * C:(i + 1) * C], h_sb[:, k, 2 * n + i, :], w("v", k), start=(k == 0), stop=(k == 1))
                        last.then_inc(a_filled("v", n), 1)
                    if g is FIRST:
                        pe.wait_ge(ld_mats.sem, 16)
                        pe.wait_ge(fills.sem, FILLS)
                        pe.wait_ge(ld_w[1].sem, 16)
                        for m in range(2):
                            for k in range(2):
                                last = mm(red_ps[:, m:m + 1], w("o", k, m * P, m * P + P), v("v_b", k), start=(k == 0), stop=(k == 1))
                        last.then_inc(bias_sum.sem, 1)
                        pe.wait_ge(folded.sem, FOLDS)
                    pe.wait_ge(mask_made.sem, count(mask_made, g, 1))
                elif piece[0] == "u":
                    s = int(piece[1:])
                    if s == 0:
                        for n in range(2):
                            pe.wait_ge(*a_taken(g, "k", 1, n))
                    if s < UNITS:
                        scores(g, s)
                    if 2 <= s <= UNITS + 1:
                        transpose(g, s - 2)
                    if s == 3:
                        for n in (2, 3):
                            pe.wait_ge(*a_taken(g, "v", n))
                    if s >= 3:
                        values(g, s - 3)
                elif piece == "o":
                    pe.wait_ge(o_free.sem, count(o_free, g, 4))
                    for m in range(2):
                        bank = a_bank("o", m)
                        pe.wait_ge(*a_open(g, "o", m))
                        project(bank, "o", m, [attn[:, :, k, :] for k in range(2)]).then_inc(a_filled("o", m), 1)
                elif piece == "rms":
                    pe.wait_ge(ysq_made.sem, count(ysq_made, g, 1))
                    bank = a_bank("rms")
                    pe.wait_ge(*a_open(g, "rms"))
                    average(bank, ysq).then_inc(a_filled("rms"), 1)
                elif piece in ("mlp0", "mlp1", "x1"):
                    if piece == "mlp0":
                        pe.wait_ge(yn_made.sem, count(yn_made, g, 1))
                        if g is FIRST:
                            pe.wait_ge(ld_w2.sem, 16)
                    for m in {"mlp0": range(0, 4), "mlp1": range(4, 8), "x1": range(8, 9)}[piece]:
                        if m < FM:
                            bank = a_bank("w1", m)
                            pe.wait_ge(*a_open(g, "w1", m))
                            project(bank, "w1", m, [y[:, k, :] for k in range(2)]).then_inc(a_filled("w1", m), 1)
                        if m == 1:
                            pe.wait_ge(pt_free.sem, count(pt_free, g, UNITS))
                            pe.wait_ge(o_free.sem, count(o_free, g, 4))
                        if m >= 1:
                            pe.wait_ge(*a_taken(g, "w1", m - 1))
                            a = mm(pt_ps[:, :], w2_sb[:, m - 1, 0:P], hid[:, (m - 1) % 2, :], start=(m == 1), stop=(m == FM))
                            b = mm(o_ps[:, :], w2_sb[:, m - 1, P:C], hid[:, (m - 1) % 2, :], start=(m == 1), stop=(m == FM))
                    if piece == "x1":
                        a.then_inc(pt_full.sem, 1)
                        b.then_inc(o_full.sem, 1)

            def gather(g, h, j):
                if j == 0:
                    pe.wait_ge(red_free.sem, count(red_free, g, h))
                pe.wait_ge(rs_made.sem, count(rs_made, g, h * RH + j + 1))
                return mm(red_ps[:, :], mat(f"gather{j}"), rs[:, j % 2, :], start=(j == 0), stop=False)

            def recurrent(g, piece):
                if piece in ("mean0", "mean1"):
                    n = int(piece[-1])
                    if n == 0:
                        pe.wait_ge(pt_free.sem, count(pt_free, g, UNITS + 1))
                        pe.wait_ge(o_free.sem, count(o_free, g, 5))
                    else:
                        for m in range(2):
                            pe.wait_ge(*r_taken(g, "O", m))
                    bank = r_bank("mean", n)
                    pe.wait_ge(*r_open(g, "mean", n))
                    average(bank, (x1, x2)[n]).then_inc(r_filled("mean", n), 1)
                elif piece in ("var0", "var1"):
                    n = int(piece[-1])
                    pe.wait_ge(sq_made.sem, count(sq_made, g, n + 1))
                    bank = r_bank("var", n)
                    pe.wait_ge(*r_open(g, "var", n))
                    average(bank, sq).then_inc(r_filled("var", n), 1)
                elif piece == "maa":
                    pe.wait_ge(ld_w[2].sem, 16)
                    pe.wait_ge(ld_small.sem, 32)
                    pe.wait_ge(z_made.sem, count(z_made, g, 2))
                    for m, width in ((0, P), (1, DM)):
                        bank = r_bank("maa", m)
                        pe.wait_ge(*r_open(g, "maa", m))
                        project(bank, "maa1", m, [xm[:, 1, k, :] for k in range(2)], width).then_inc(r_filled("maa", m), 1)
                elif piece[0] == "x":
                    n = int(piece[1])
                    if n in (0, 4):
                        pe.wait_ge(*r_taken(g, "maa", n // 4))
                    for m in range(2):
                        bank = r_bank("x", n, m)
                        pe.wait_ge(*r_open(g, "x", n, m))
                        mm(bank[:, :], maa2_sb[:, ORDER[n], m * P:(m + 1) * P], th[:, ORDER[n] // 4, :], start=True, stop=True).then_inc(r_filled("x", n, m), 1)
                    if n >= 1:
                        pe.wait_ge(xm_made.sem, count(xm_made, g, 2 * n))
                    shifted = [xm[:, (n - 1) % 2, k, :] for k in range(2)]
                    if n == 1:
                        bank = r_bank("td1")
                        pe.wait_ge(*r_open(g, "td1"))
                        project(bank, "td1", 0, shifted, DD).then_inc(r_filled("td1"), 1)
                    if n == 2:
                        pe.wait_ge(*r_taken(g, "td1"))
                        for m in range(2):
                            bank = r_bank("td2", m)
                            pe.wait_ge(*r_open(g, "td2", m))
                            mm(bank[:, :], td2_sb[:, m * P:(m + 1) * P], tw[:, :], start=True, stop=True).then_inc(r_filled("td2", m), 1)
                    if n >= 2:
                        to = {2: "K", 3: "V", 4: "R"}[n]
                        for m in range(2):
                            bank = r_bank(to, m)
                            pe.wait_ge(*r_open(g, to, m))
                            project(bank, "W" + to.lower(), m, shifted).then_inc(r_filled(to, m), 1)
                elif piece == "G":
                    pe.wait_ge(xm_made.sem, count(xm_made, g, 2 * MIX))
                    for m in range(2):
                        bank = r_bank("G", m)
                        pe.wait_ge(*r_open(g, "G", m))
                        project(bank, "Wg", m, [xm[:, 0, k, :] for k in range(2)]).then_inc(r_filled("G", m), 1)
                elif piece[0:2] in ("s0", "s1") and len(piece) == 3:
                    h, q = int(piece[1]), int(piece[2])
                    if h == 0 and q == 0:
                        for m in range(2):
                            pe.wait_ge(*r_taken(g, "V", m))
                    for j in (2 * q, 2 * q + 1):
                        bank = r_bank("spread", h, j)
                        pe.wait_ge(*r_open(g, "spread", h, j))
                        mm(bank[:, :], mat(f"spread{j}"), vr[:, h, :], start=True, stop=True).then_inc(r_filled("spread", h, j), 1)
                        if j >= 1:
                            gather(g, h, j - 1)
                    if (h, q) == (1, 1):
                        variance(g, 0)
                    if q == 3:
                        pe.wait_ge(rk_made.sem, count(rk_made, g, h + 1))
                        bank = r_bank("coef", h)
                        pe.wait_ge(*r_open(g, "coef", h))
                        mm(bank[:, :], bonus_w[:, h, :], rk[:, :], start=True, stop=True).then_inc(r_filled("coef", h), 1)
                        gather(g, h, RH - 1)
                        pe.wait_ge(*r_taken(g, "coef", h))
                        mm(red_ps[:, :], mat("center8"), bonus[:, :], start=False, stop=True).then_inc(red_full.sem, 1)
                elif piece == "gn":
                    variance(g, 1)
                elif piece == "O":
                    pe.wait_ge(gn3_made.sem, count(gn3_made, g, 2))
                    for m in range(2):
                        bank = r_bank("O", m)
                        pe.wait_ge(*r_open(g, "O", m))
                        project(bank, "Wo", m, [og[:, k, :] for k in range(2)]).then_inc(r_filled("O", m), 1)
                elif piece == "ffn":
                    for n, to in enumerate(("fk", "fr")):
                        pe.wait_ge(shift_made.sem, count(shift_made, g, 2 * n + 2))
                        for m in range(2):
                            bank = r_bank(to, m)
                            pe.wait_ge(*r_open(g, to, m))
                            project(bank, "W" + to, m, [xm[:, n, k, :] for k in range(2)]).then_inc(r_filled(to, m), 1)
                    pe.wait_ge(act_made.sem, count(act_made, g, 2))
                    for m in range(2):
                        bank = r_bank("fv", m)
                        pe.wait_ge(*r_open(g, "fv", m))
                        project(bank, "Wfv", m, [act[:, k, :] for k in range(2)]).then_inc(r_filled("fv", m), 1)

            def variance(g, h):
                pe.wait_ge(red_free.sem, count(red_free, g, h + 1))
                bank = r_bank("gvar", h)
                pe.wait_ge(*r_open(g, "gvar", h))
                mm(bank[:, :], mat("mean8"), gsq[:, h, :], start=True, stop=True).then_inc(r_filled("gvar", h), 1)

            run(pe, attention, recurrent)

        @block.scalar
        def _(sc):
            act_fn = nc.scalar.activation

            def attention(g, piece):
                if piece == "qk":
                    if g is FIRST:
                        sc.wait_ge(ld_vec.sem, 16)
                    for m in range(2):
                        for n in range(2):
                            bank = a_bank("k", m, n)
                            sc.wait_ge(*a_ready(g, "k", m, n))
                            ins = act_fn(kt[:, m, 4 * n:4 * n + 4, :].rearrange("p b s -> p (b s)"), bank[:, :], ACT.Identity, bias=v("k_b", m))
                            ins.then_inc(a_read("k", m, n), 1)
                elif piece == "v":
                    for n in range(4):
                        bank = a_bank("v", n)
                        sc.wait_ge(*a_ready(g, "v", n))
                        ins = act_fn(vv[:, 2 * n:2 * n + 2, :].rearrange("p b s -> p (b s)"), bank[:, :], ACT.Copy)
                        ins.then_inc(a_read("v", n), 1)
                elif piece[0] == "u":
                    s = int(piece[1:])
                    if s < UNITS:
                        sc.wait_ge(max_made.sem, count(max_made, g, s + 1))
                        sc.wait_ge(norm_made.sem, count(norm_made, g, max(s - 1, 0)))
                        sc.wait_ge(pt_full.sem, count(pt_full, g, max(s - 2, 0)))
                        bank = A_BANK[A_SLOT[("s", s)][0]]
                        for n in range(4):
                            ins = act_fn(probs[:, s % 3, n, :], bank[:, n * P:(n + 1) * P], ACT.Exp,
                                         bias=neg_max[:, s % 2, n:n + 1], accum_out=sums[:, s % 2, n:n + 1])
                        ins.then_inc(a_read("s", s), 1)
                    if s >= 6 and (s - 6) % 4 == 0:
                        bp = (s - 6) // 4
                        sc.wait_ge(o_full.sem, count(o_full, g, bp + 1))
                        sc.wait_ge(o_free.sem, count(o_free, g, bp))
                        act_fn(o_even[:, :, :], o_ps[:, :].rearrange("p (n e s) -> p n e s", n=4, e=2)[:, :, 0, :], ACT.Copy, scale=v("even")).then_inc(o_even_made.sem, 1)
                elif piece == "o":
                    for m in range(2):
                        sc.wait_ge(*a_taken(g, "o", m))
                    act_fn(ysq, y[:, :, :], ACT.Square).then_inc(ysq_made.sem, 1)
                elif piece == "rms":
                    bank = a_bank("rms")
                    sc.wait_ge(*a_ready(g, "rms"))
                    act_fn(a_ms[:, :], bank[:, :], ACT.Sqrt, bias=v("eps6")).then_inc(a_read("rms"), 1)
                elif piece in ("mlp0", "mlp1"):
                    for m in range(0, 4) if piece == "mlp0" else range(4, 8):
                        bank = a_bank("w1", m)
                        sc.wait_ge(*a_ready(g, "w1", m))
                        ins = act_fn(hid[:, m % 2, :], bank[:, :], ACT.Gelu_apprx_tanh, bias=v("b1", m))
                        ins.then_inc(a_read("w1", m), 1)

            def recurrent(g, piece):
                if piece in ("mean0", "mean1"):
                    n = int(piece[-1])
                    sc.wait_ge(*r_taken(g, "mean", n))
                    act_fn(sq[:, :, :], xc[:, :, :], ACT.Square).then_inc(sq_made.sem, 1)
                    sc.wait_ge(st_in.sem, count(st_in, g, 16))
                    sc.wait_ge(sx_made.sem, count(sx_made, g, n))
                    act_fn(xs[:, :, :, 0], st_sb[:, 1 - n, :, :], ACT.Copy).then_inc(row_made.sem, 1)
                elif piece in ("var0", "var1"):
                    bank = r_bank("var", int(piece[-1]))
                    sc.wait_ge(*r_ready(g, "var", int(piece[-1])))
                    act_fn(r_ms[:, :], bank[:, :], ACT.Sqrt, bias=v("eps5")).then_inc(r_read("var", int(piece[-1])), 1)
                elif piece == "maa":
                    for m, width in ((0, P), (1, DM)):
                        bank = r_bank("maa", m)
                        sc.wait_ge(*r_ready(g, "maa", m))
                        ins = act_fn(th[0:width, m, :], bank[0:width, :], ACT.Tanh)
                        ins.then_inc(r_read("maa", m), 1)
                elif piece == "x1":
                    bank = r_bank("td1")
                    sc.wait_ge(*r_ready(g, "td1"))
                    ins = act_fn(tw[0:DD, :], bank[0:DD, :], ACT.Tanh)
                    ins.then_inc(r_read("td1"), 1)
                elif piece == "x2":
                    for m in range(2):
                        bank = r_bank("td2", m)
                        sc.wait_ge(*r_ready(g, "td2", m))
                        ins = act_fn(e1[:, m, :], bank[:, :], ACT.Exp, bias=v("td", m))
                        ins.then_inc(r_read("td2", m), 1)
                    for m in range(2):
                        sc.wait_ge(*r_taken(g, "td2", m))
                        act_fn(decay[:, m, :, 1:S], by_batch(e1[:, m, :])[:, :, 0:S - 1], ACT.Exp, scale=-1.0).then_inc(decay_made.sem, 1)
                    copy(g, "K", kk)
                elif piece == "x3":
                    copy(g, "V", vr)
                elif piece == "x4":
                    copy(g, "R", rr)
                elif piece == "G":
                    for m in range(2):
                        bank = r_bank("G", m)
                        sc.wait_ge(*r_ready(g, "G", m))
                        act_fn(gt[:, m, :], bank[:, :], ACT.Tanh, scale=0.5).then_inc(gt_made.sem, 1)
                elif piece[0:2] in ("s0", "s1") and len(piece) == 3:
                    h, q = int(piece[1]), int(piece[2])
                    turn = 4 * h + q
                    if turn == 0:
                        sc.wait_ge(s0_in.sem, count(s0_in, g, 16))
                    sc.wait_ge(st_made.sem, count(st_made, g, max(0, 2 * turn - 2)))
                    a = 2 * q % 4
                    act_fn(kv[:, a:a + 2, :, 0], s0_sb[:, h, 2 * q:2 * q + 2, :], ACT.Copy).then_inc(first_made.sem, 1)
                    if (h, q) == (1, 0):
                        take(g, 0)
                    if (h, q) == (1, 1):
                        deviation(g, 0)
                elif piece == "gn":
                    take(g, 1)
                    deviation(g, 1)
                elif piece == "ffn":
                    for m in range(2):
                        bank = r_bank("fk", m)
                        sc.wait_ge(*r_ready(g, "fk", m))
                        ins = act_fn(relu[:, m, :], bank[:, :], ACT.Relu)
                        ins.then_inc(r_read("fk", m), 1)
                    for m in range(2):
                        bank = r_bank("fr", m)
                        sc.wait_ge(*r_ready(g, "fr", m))
                        ins = act_fn(tr[:, m, :], bank[:, :], ACT.Tanh, scale=0.5)
                        ins.then_inc(r_read("fr", m), 1)

            def copy(g, name, to):
                for m in range(2):
                    bank = r_bank(name, m)
                    sc.wait_ge(*r_ready(g, name, m))
                    ins = act_fn(to[:, m, :], bank[:, :], ACT.Copy)
                    ins.then_inc(r_read(name, m), 1)

            def take(g, h):
                sc.wait_ge(red_full.sem, count(red_full, g, h + 1))
                if h == 0:
                    for m in range(2):
                        sc.wait_ge(*r_taken(g, "G", m))
                act_fn(og[:, h, :], red_ps[:, :], ACT.Copy).then_inc(og_made.sem, 1)
                ins = act_fn(gsq[:, h, :], red_ps[:, :], ACT.Square)
                ins.then_inc(red_free.sem, 1)

            def deviation(g, h):
                bank = r_bank("gvar", h)
                sc.wait_ge(*r_ready(g, "gvar", h))
                if h == 0:
                    sc.wait_ge(xm_made.sem, count(xm_made, g, 2 * MIX))
                act_fn(g_ms[:, h, :], bank[:, :], ACT.Sqrt, bias=v("eps5")).then_inc(r_read("gvar", h), 1)

            run(sc, attention, recurrent)

        @block.vector
        def _(ve):
            tt, ts, stt = nc.vector.tensor_tensor, nc.vector.tensor_scalar, nc.vector.scalar_tensor_tensor

            def normalise(g, n):
                ve.wait_ge(*r_taken(g, "var", n))
                nc.vector.reciprocal(r_ms[:, :], r_ms[:, :]).then_inc(rstd_made.sem, 1)
                ve.wait_ge(rstd_made.sem, count(rstd_made, g, n + 1))
                tt(xc[:, :, :], xc[:, :, :], both(r_ms[:, :]), ALU.mult).then_inc(xn_made.sem, 1)
                ve.wait_ge(xn_made.sem, count(xn_made, g, n + 1))
                name = ("ln1", "ln2")[n]
                for h in range(2):
                    ts(xs[:, h, :, 1:S + 1], by_batch(xc[:, h, :]), v(name + "_w", h), v(name + "_b", h), ALU.mult, ALU.add).then_inc(xs_made.sem, 1)
                ve.wait_ge(xs_made.sem, count(xs_made, g, 2 * n + 2))
                ve.wait_ge(row_made.sem, count(row_made, g, n + 1))
                for h in range(2):
                    ins = tt(by_batch(sx[:, h, :]), xs[:, h, :, 0:S], xs[:, h, :, 1:S + 1], ALU.subtract)
                ins.then_inc(sx_made.sem, 1)
                ve.wait_ge(sx_made.sem, count(sx_made, g, n + 1))

            def shift(g, to, name, h, event):
                stt(by_batch(xm[:, to, h, :]), by_batch(sx[:, h, :]), v(name, h), xs[:, h, :, 1:S + 1], ALU.mult, ALU.add).then_inc(event.sem, 1)

            def attention(g, piece):
                if piece == "qk":
                    if g is FIRST:
                        ve.wait_ge(ld_vec.sem, 16)
                        for e, name in enumerate(("even16", "odd16")):
                            ts(q_bias[:, e, :], vec[:, V_COLS["q_b"]:V_COLS["q_b"] + 2], v(name), None, ALU.mult).then_inc(folded.sem, 1)
                        ve.wait_ge(folded.sem, 2)
                    for m in range(2):
                        bank = a_bank("q", m)
                        ve.wait_ge(*a_ready(g, "q", m))
                        for e, name in enumerate(("even16", "odd16")):
                            ins = ts(qt[:, m, :, e, :], by_batch(bank[:, :]), v(name), q_bias[:, e, m:m + 1], ALU.mult, ALU.add)
                        ins.then_inc(a_read("q", m), 1)
                    ve.wait_ge(mask_in.sem, count(mask_in, g, 16))
                    ts(mask_b[:, :, :], mask_i[:, :, :], 0, NEG, ALU.is_equal, ALU.mult).then_inc(mask_made.sem, 1)
                elif piece == "v":
                    if g is FIRST:
                        ve.wait_ge(ld_w[1].sem, 16)
                        for k in range(2):
                            ts(w("w1", k), w("w1", k), v("pn", k), None, ALU.mult).then_inc(folded.sem, 1)
                        ve.wait_ge(bias_sum.sem, 1)
                        tt(o_bias[:, :], red_ps[:, 0:2], vec[:, V_COLS["o_b"]:V_COLS["o_b"] + 2], ALU.add).then_inc(folded.sem, 1)
                        ve.wait_ge(ld_mats.sem, 16)
                        for k in range(2):
                            ts(bonus_w[:, k, :], mat("same_head"), v("u", k), None, ALU.mult).then_inc(folded.sem, 1)
                        ve.wait_ge(ld_w[2].sem, 16)
                        for name in ("Wo", "Wfv"):
                            for k in range(2):
                                ts(w(name, k), w(name, k), 0.5, None, ALU.mult).then_inc(folded.sem, 1)
                        ve.wait_ge(folded.sem, FOLDS)
                elif piece[0] == "u":
                    s = int(piece[1:])
                    if 1 <= s <= UNITS:
                        ve.wait_ge(*a_taken(g, "s", s - 1))
                        nc.vector.reciprocal(rsum[:, (s - 1) % 2, :], sums[:, (s - 1) % 2, :]).then_inc(rsum_made.sem, 1)
                    if s < UNITS:
                        bank = a_bank("s", s)
                        ve.wait_ge(*a_ready(g, "s", s))
                        nc.vector.tensor_reduce(neg_max[:, s % 2, :], bank[:, :].rearrange("p (n k) -> p n k", n=4), AX.X, ALU.max, negate=True).then_inc(max_made.sem, 1)
                    if 2 <= s <= UNITS + 1:
                        ve.wait_ge(pt_full.sem, count(pt_full, g, s - 1))
                        ins = nc.vector.tensor_copy(probs_t[:, s % 2, :, :].rearrange("p n q -> p (n q)"), pt_ps[:, :])
                        ins.then_inc(pt_free.sem, 1)
                    if s >= 6 and (s - 6) % 4 == 0:
                        bp = (s - 6) // 4
                        ve.wait_ge(o_even_made.sem, count(o_even_made, g, bp + 1))
                        ins = stt(attn[:, 2 * bp:2 * bp + 2, :, :].rearrange("p b h s -> p (b h) s"),
                                  o_ps[:, :].rearrange("p (n e s) -> p n e s", n=4, e=2)[:, :, 1, :], v("odd"), o_even[:, :, :], ALU.mult, ALU.add)
                        ins.then_inc(o_free.sem, 1)
                elif piece == "o":
                    ve.wait_ge(xa_in.sem, count(xa_in, g, 16))
                    for m in range(2):
                        bank = a_bank("o", m)
                        ve.wait_ge(*a_ready(g, "o", m))
                        ins = stt(y[:, m, :], bank[:, :], o_bias[:, m:m + 1], xa_sb[:, m, :], ALU.add, ALU.add)
                        ins.then_inc(a_read("o", m), 1)
                elif piece == "rms":
                    ve.wait_ge(*a_taken(g, "rms"))
                    nc.vector.reciprocal(a_ms[:, :], a_ms[:, :]).then_inc(arstd_made.sem, 1)
                    ve.wait_ge(arstd_made.sem, count(arstd_made, g, 1))
                    tt(y[:, :, :], y[:, :, :], both(a_ms[:, :]), ALU.mult).then_inc(yn_made.sem, 1)
                elif piece == "x1":
                    for m in range(2):
                        ve.wait_ge(*r_taken(g - 1, "O", m))
                    for m, (bank, full, free, n) in enumerate(((pt_ps, pt_full, pt_free, UNITS + 1), (o_ps, o_full, o_free, 5))):
                        ve.wait_ge(full.sem, count(full, g, n))
                        ins = stt(x1[:, m, :], bank[:, :], v("b2", m), xa_sb[:, m, :], ALU.add, ALU.add)
                        ins.then_inc(free.sem, 1)

            def recurrent(g, piece):
                if piece in ("mean0", "mean1"):
                    n = int(piece[-1])
                    bank = r_bank("mean", n)
                    ve.wait_ge(*r_ready(g, "mean", n))
                    if n == 0:
                        ve.wait_ge(pt_free.sem, count(pt_free, g, UNITS + 1))
                        ve.wait_ge(o_free.sem, count(o_free, g, 5))
                    ins = tt(xc[:, :, :], (x1, x2)[n][:, :, :], both(bank[:, :]), ALU.subtract)
                    ins.then_inc(r_read("mean", n), 1)
                elif piece == "maa":
                    normalise(g, 0)
                    for h in range(2):
                        shift(g, 1, "maa_x", h, z_made)
                elif piece[0] == "x":
                    n = int(piece[1])
                    if n == 0:
                        ve.wait_ge(fin_made.sem, count(fin_made, g, 0))
                    for h in range(2):
                        bank = r_bank("x", n, h)
                        ve.wait_ge(*r_ready(g, "x", n, h))
                        ve.wait_ge(xm_made.sem, count(xm_made, g, max(0, 2 * n + h - 1)))
                        ins = stt(tmp[:, h, :], bank[:, :], v("maa", 2 * ORDER[n] + h), sx[:, h, :], ALU.add, ALU.mult)
                        ins.then_inc(r_read("x", n, h), 1)
                elif piece == "G":
                    for h in range(2):
                        ve.wait_ge(gt_made.sem, count(gt_made, g, h + 1))
                        ins = stt(gate[:, h, :], gt[:, h, :], 1.0, R_BANK[R_SLOT[("G", h)][0]][:, :], ALU.add, ALU.mult)
                        ins.then_inc(r_read("G", h), 1)
                elif piece[0:2] in ("s0", "s1") and len(piece) == 3:
                    h, q = int(piece[1]), int(piece[2])
                    for j in (2 * q, 2 * q + 1):
                        n = h * RH + j
                        if n == 0:
                            for m in range(2):
                                ve.wait_ge(*r_taken(g, "K", m))
                            ve.wait_ge(decay_made.sem, count(decay_made, g, 2))
                        bank = r_bank("spread", h, j)
                        ve.wait_ge(*r_ready(g, "spread", h, j))
                        ins = tt(kv[:, j % 4, :, 1:S], by_batch(bank[:, :])[:, :, 0:S - 1], by_batch(kk[:, h, :])[:, :, 0:S - 1], ALU.mult)
                        ins.then_inc(r_read("spread", h, j), 1)
                        ve.wait_ge(*r_taken(g, "spread", h, j))
                        ve.wait_ge(first_made.sem, count(first_made, g, n // 2 + 1))
                        ve.wait_ge(rs_made.sem, count(rs_made, g, max(0, n - 1)))
                        nc.vector.tensor_tensor_scan(st[:, j % 2, :], decay[:, h, :, :].rearrange("p b s -> p (b s)"),
                                                                                  kv[:, j % 4, :, :].rearrange("p b s -> p (b s)"), 0.0, ALU.mult, ALU.add).then_inc(st_made.sem, 1)
                    if (h, q) == (1, 2):
                        invert(g, 0)
                    if (h, q) == (1, 3):
                        scale(g, 0)
                    if q == 3:
                        bank = r_bank("coef", h)
                        ve.wait_ge(*r_ready(g, "coef", h))
                        ins = tt(bonus[:, :], bank[:, :], vr[:, h, :], ALU.mult)
                        ins.then_inc(r_read("coef", h), 1)
                elif piece == "gn":
                    invert(g, 1)
                    scale(g, 1)
                elif piece == "O":
                    ve.wait_ge(out_done.sem, count(out_done, g, 0))
                    for m in range(2):
                        bank = r_bank("O", m)
                        ve.wait_ge(*r_ready(g, "O", m))
                        ins = tt(x2[:, m, :], bank[:, :], x1[:, m, :], ALU.add)
                        ins.then_inc(r_read("O", m), 1)
                elif piece == "shift":
                    normalise(g, 1)
                    for n, name in enumerate(("fk", "fr")):
                        for h in range(2):
                            shift(g, n, name, h, shift_made)
                elif piece == "ffn":
                    for h in range(2):
                        bank = r_bank("fv", h)
                        ve.wait_ge(*r_ready(g, "fv", h))
                        ve.wait_ge(*r_taken(g, "fr", h))
                        ins = stt(tmp[:, h, :], tr[:, h, :], 1.0, bank[:, :], ALU.add, ALU.mult)
                        ins.then_inc(r_read("fv", h), 1)

            def invert(g, h):
                ve.wait_ge(*r_taken(g, "gvar", h))
                nc.vector.reciprocal(g_ms[:, h, :], g_ms[:, h, :]).then_inc(grstd_made.sem, 1)

            def scale(g, h):
                ve.wait_ge(gn1_made.sem, count(gn1_made, g, h + 1))
                ts(og[:, h, :], og[:, h, :], v("gn_w", h), v("gn_b", h), ALU.mult, ALU.add).then_inc(gn2_made.sem, 1)

            run(ve, attention, recurrent)

        @block.gpsimd
        def _(po):
            tt = nc.gpsimd.tensor_tensor
            po.memset(ones_bf[:, :], 1.0).then_inc(fills.sem, 1)
            po.memset(th[:, 1, :], 0.0).then_inc(fills.sem, 1)
            po.memset(tw[:, :], 0.0).then_inc(fills.sem, 1)
            po.memset(decay[:, :, :, 0], 0.0).then_inc(fills.sem, 1)
            po.wait_ge(fills.sem, FILLS)

            def attention(g, piece):
                if piece[0] == "u":
                    s = int(piece[1:])
                    if 1 <= s <= UNITS:
                        u = s - 1
                        po.wait_ge(rsum_made.sem, count(rsum_made, g, u + 1))
                        tt(probs[:, u % 3, :, :], probs[:, u % 3, :, :], rsum[:, u % 2, :].unsqueeze(2).broadcast_to([P, 4, KEYS]), ALU.mult).then_inc(norm_made.sem, 1)

            def recurrent(g, piece):
                if piece[0] == "x":
                    n = int(piece[1])
                    for h in range(2):
                        po.wait_ge(*r_taken(g, "x", n, h))
                        tt(by_batch(xm[:, n % 2, h, :]), by_batch(tmp[:, h, :]), xs[:, h, :, 1:S + 1], ALU.add).then_inc(xm_made.sem, 1)
                elif piece[0:2] in ("s0", "s1") and len(piece) == 3:
                    h, q = int(piece[1]), int(piece[2])
                    if q == 0:
                        po.wait_ge(*r_taken(g, "K", h))
                        po.wait_ge(*r_taken(g, "R", h))
                        po.wait_ge(red_full.sem, count(red_full, g, h))
                        tt(rk[:, :], rr[:, h, :], kk[:, h, :], ALU.mult).then_inc(rk_made.sem, 1)
                    for j in (2 * q, 2 * q + 1):
                        po.wait_ge(st_made.sem, count(st_made, g, h * RH + j + 1))
                        tt(rs[:, j % 2, :], st[:, j % 2, :], rr[:, h, :], ALU.mult).then_inc(rs_made.sem, 1)
                    if (h, q) == (1, 2):
                        grow(g, 0)
                    if (h, q) == (1, 3):
                        gated(g, 0)
                elif piece == "gn":
                    grow(g, 1)
                    gated(g, 1)
                elif piece == "ffn":
                    for h in range(2):
                        po.wait_ge(*r_taken(g, "fk", h))
                        tt(act[:, h, :], relu[:, h, :], relu[:, h, :], ALU.mult).then_inc(act_made.sem, 1)
                    for h in range(2):
                        po.wait_ge(*r_taken(g, "fv", h))
                        tt(x2[:, h, :], x2[:, h, :], tmp[:, h, :], ALU.add).then_inc(fin_made.sem, 1)

            def grow(g, h):
                po.wait_ge(grstd_made.sem, count(grstd_made, g, h + 1))
                po.wait_ge(og_made.sem, count(og_made, g, h + 1))
                tt(og[:, h, :], og[:, h, :], g_ms[:, h, :], ALU.mult).then_inc(gn1_made.sem, 1)

            def gated(g, h):
                po.wait_ge(gn2_made.sem, count(gn2_made, g, h + 1))
                if h == 0:
                    for m in range(2):
                        po.wait_ge(*r_taken(g, "G", m))
                tt(og[:, h, :], og[:, h, :], gate[:, h, :], ALU.mult).then_inc(gn3_made.sem, 1)

            run(po, attention, recurrent)


FILLS, FOLDS = 4, 11


def unit(u):
    return u // PAIRS, u % PAIRS


def kernel(**inputs):
    import numpy as np
    import concourse.bacc as bacc
    from concourse import mybir as my
    from concourse.bass_utils import run_bass_kernel_spmd

    a = {n: np.asarray(x) for n, x in inputs.items()}
    l0 = {n[len("L0_xattn_"):]: x for n, x in a.items() if n.startswith("L0_xattn_")}
    l1 = {n[len("L1_xattn_"):]: x for n, x in a.items() if n.startswith("L1_xattn_")}
    x, ctx = a["x"], a["ctx_2048"]

    def halves(m):
        return m.reshape(HALVES, P, -1).transpose(1, 0, 2)

    def grouped(z):
        return z.reshape(GROUPS, GB, z.shape[1], HALVES, P).transpose(0, 4, 3, 1, 2)

    kv_w = l0["kv_w"].reshape(C, C, 2)
    kv_b = l0["kv_b"].reshape(C, 2)
    weights = {"q": l0["q_w"], "k": kv_w[:, :, 0], "v": kv_w[:, :, 1], "o": l0["out_w"], "w1": l0["mlp_w1"],
               "maa1": l1["maa_w1"], "td1": l1["td_w1"], "Wr": l1["Wr"].T, "Wk": l1["Wk"].T, "Wv": l1["Wv"].T, "Wg": l1["Wg"].T,
               "Wo": l1["Wo"].T, "Wfk": l1["Wfk"].T, "Wfr": l1["Wfr"].T, "Wfv": l1["Wfv"].T}
    parity = (np.arange(P) // DH) % 2
    even, odd = (parity == 0).astype(np.float32), (parity == 1).astype(np.float32)
    vectors = {"q_b": l0["q_b"], "k_b": kv_b[:, 0], "v_b": kv_b[:, 1], "o_b": l0["out_b"], "pn": l0["postnorm_w"], "b1": l0["mlp_b1"],
               "b2": l0["mlp_b2"], "ln1_w": l1["ln1_w"], "ln1_b": l1["ln1_b"], "ln2_w": l1["ln2_w"], "ln2_b": l1["ln2_b"],
               "maa_x": l1["maa_x"], "maa": l1["maa_stack"].reshape(-1), "td": l1["time_decay"], "gn_w": l1["gn_w"], "gn_b": l1["gn_b"],
               "fk": l1["ffn_maa_k"], "fr": l1["ffn_maa_r"], "u": l1["u"].reshape(-1),
               "even": even, "odd": odd, "even16": even / np.float32(DH), "odd16": odd / np.float32(DH),
               "eps6": np.full(P, 1e-6, np.float32), "eps5": np.full(P, 1e-5, np.float32)}
    p = np.arange(P)
    same = (p[:, None] // RH == p[None, :] // RH).astype(np.float32)
    center = np.eye(P, dtype=np.float32) - same / np.float32(RH)
    mats = {"ident": np.eye(P, dtype=np.float32), "mean256": np.full((P, P), 1 / C, np.float32), "mean8": same / np.float32(RH),
            "center8": center, "same_head": same}
    for j in range(RH):
        pick = same * (p[:, None] % RH == j)
        mats[f"spread{j}"] = pick.astype(np.float32)
        mats[f"gather{j}"] = (same * ((p[None, :] % RH == j) - np.float32(1 / RH))).astype(np.float32)
    maa2 = np.zeros((P, MIX, C), np.float32)
    for f in range(MIX):
        row = DM * f % P
        maa2[row:row + DM, f, :] = l1["maa_w2"][f]
    td2 = np.zeros((P, C), np.float32)
    td2[0:DD] = l1["td_w2"]
    arrays = {
        "hT": grouped(np.concatenate([ctx, x], axis=1)),
        "xT": grouped(x).reshape(GROUPS, P, HALVES, T),
        "maskT": a["mask_BxS2_ik0"].reshape(GROUPS, T),
        "stT": grouped(ctx[:, 0:2]).transpose(0, 1, 4, 2, 3),
        "s0T": ctx[:, 2:2 + RH].reshape(GROUPS, GB, HALVES, P, RH).transpose(0, 3, 2, 4, 1),
        "W": np.concatenate([halves(weights[n]) for n in W_COLS], axis=2),
        "W2": l0["mlp_w2"].reshape(FM, P, C).transpose(1, 0, 2),
        "MAA2": maa2,
        "TD2": td2,
        "VEC": np.concatenate([vectors[n].reshape(-1, P).T for n in V_COLS], axis=1),
        "MATS": np.stack([mats[n] for n in M_NAMES], axis=1),
    }
    nc = bacc.Bacc("TRN2", target_bir_lowering=False, num_devices=1)
    arrays = {n: np.ascontiguousarray(z) for n, z in arrays.items()}
    args = {n: nc.dram_tensor(n, list(z.shape), my.dt.from_np(z.dtype), kind="ExternalInput").ap() for n, z in arrays.items()}
    out = nc.dram_tensor("out", [GROUPS, P, HALVES, T], my.dt.float32, kind="ExternalOutput").ap()
    build(nc, *[args[n] for n in ("hT", "xT", "maskT", "stT", "s0T", "W", "W2", "MAA2", "TD2", "VEC", "MATS")], out)
    r = run_bass_kernel_spmd(nc, [arrays], core_ids=[0])
    got = r.results[0]["out"]
    return got.reshape(GROUPS, P, HALVES, GB, S).transpose(0, 3, 4, 2, 1).reshape(B, S, C)
```

```python
import concourse.bass as bass
from concourse import mybir
from contextlib import ExitStack

B, S, C = 64, 64, 256
P = 128
HALVES = C // P
GB = 4
GROUPS = B // GB
T = GB * S
KEYS = 2 * S
HEADS, DH = 16, 16
PAIRS = P // (2 * DH)
UNITS = (GB // 2) * PAIRS
F = 4 * C
FM = F // P
RH = 8
DM, DD = 32, 64
MIX = 5
ORDER = (1, 0, 2, 3, 4)
FIRST = 0
NEG = -1e30

W_COLS = {}
at = 0
for _name, _n in (("q", C), ("k", C), ("v", C), ("o", C), ("w1", F), ("maa1", MIX * DM), ("td1", DD),
                  ("Wr", C), ("Wk", C), ("Wv", C), ("Wg", C), ("Wo", C), ("Wfk", C), ("Wfr", C), ("Wfv", C)):
    W_COLS[_name] = (at, at + _n)
    at += _n
W_TOTAL = at
W_PARTS = (("q", "v"), ("o", "w1"), ("maa1", "Wfv"))

V_COLS = {}
at = 0
for _name, _n in (("q_b", 2), ("k_b", 2), ("v_b", 2), ("o_b", 2), ("pn", 2), ("b1", FM), ("b2", 2), ("ln1_w", 2), ("ln1_b", 2),
                  ("ln2_w", 2), ("ln2_b", 2), ("maa_x", 2), ("maa", 2 * MIX), ("td", 2), ("gn_w", 2), ("gn_b", 2),
                  ("fk", 2), ("fr", 2), ("u", 2), ("even", 1), ("odd", 1), ("even16", 1), ("odd16", 1), ("eps6", 1), ("eps5", 1)):
    V_COLS[_name] = at
    at += _n
V_TOTAL = at

M_NAMES = ["ident", "mean256", "mean8", "center8", "same_head"] + [f"gather{j}" for j in range(RH)]
M_COL = {n: i for i, n in enumerate(M_NAMES)}


def slots(names, banks):
    return {n: (banks[i], banks[:i].count(banks[i])) for i, n in enumerate(names)}, [banks.count(b) for b in range(max(banks) + 1)]


A_NAMES = ([("q",), ("k", 0), ("k", 1), ("v", 0), ("v", 1)] + [("s", u) for u in range(UNITS)]
           + [("o",), ("rms",)] + [("w1", n) for n in range(FM // 2)])
A_BANKS = [1, 0, 1, 0, 1] + [u % 2 for u in range(UNITS)] + [0, 0, 1, 0, 1, 0]
A_SLOT, A_USES = slots(A_NAMES, A_BANKS)
R_NAMES = ([("mean", 0), ("var", 0), ("maa",), ("x", 0), ("x", 1), ("td1",), ("x", 2), ("td2",), ("K",), ("x", 3), ("V",),
            ("x", 4), ("R",), ("G",)] + [("coef",), ("gvar",), ("O",), ("mean", 1), ("var", 1), ("fk",), ("fr",), ("fv",)])
R_SLOT, R_USES = slots(R_NAMES, [i % 3 for i in range(len(R_NAMES))])

TURN = [("R", "mean0"), ("A", "u4"), ("R", "var0"), ("A", "u5"), ("R", "norm0"), ("A", "u6"), ("R", "maa"), ("A", "u7"),
        ("A", "u8"), ("R", "x0"), ("A", "u9"), ("R", "x1"), ("A", "u10"), ("R", "x2"), ("R", "x3"), ("R", "x4"), ("A", "o"),
        ("A", "rms"), ("R", "G"), ("R", "s0"), ("A", "mlp0"), ("A", "mlp1"), ("R", "s1"), ("R", "s2"), ("R", "s3"),
        ("R", "s4"), ("R", "s5"), ("A", "mlp2"), ("R", "s6"), ("A", "mlp3"), ("R", "s7"), ("R", "s8"), ("R", "s9"),
        ("N", "q"), ("R", "gn"), ("N", "k"), ("N", "v0"), ("N", "v1"), ("N", "u0"), ("R", "O"), ("R", "mean1"),
        ("R", "var1"), ("R", "norm1"), ("N", "u1"), ("A", "x1"), ("R", "fk"), ("R", "fr"), ("N", "u2"), ("R", "fv"),
        ("N", "u3")]


def build(nc, hT, xT, maskT, stT, s0T, W, W2, MAA2, TD2, VEC, MATS, out):
    fp32, bf16, i32 = mybir.dt.float32, mybir.dt.bfloat16, mybir.dt.int32
    ALU, ACT, AX = mybir.AluOpType, mybir.ActivationFunctionType, mybir.AxisListType

    with ExitStack() as ctx:
        def sb(name, shape, dt=fp32):
            return ctx.enter_context(nc.sbuf_tensor(name, shape, dt))

        class Event:
            def __init__(self, name, per_group):
                self.sem, self.n = ctx.enter_context(nc.semaphore(name)), per_group

        def count(event, g, k):
            value = g * event.n + k
            return max(value, 0) if isinstance(value, int) else value

        w_sb = sb("w_sb", [P, HALVES, W_TOTAL])
        w2_sb = sb("w2_sb", [P, FM, C])
        maa2_sb = sb("maa2_sb", [P, MIX, C])
        td2_sb = sb("td2_sb", [P, C])
        vec = sb("vec", [P, V_TOTAL])
        mats = sb("mats", [P, len(M_NAMES), P])
        bonus_w = sb("bonus_w", [P, HALVES, P])
        q_bias = sb("q_bias", [P, 2, HALVES])
        o_bias = sb("o_bias", [P, HALVES])
        ones_bf = sb("ones_bf", [P, P], bf16)

        def w(name, k, a=0, b=None):
            lo, hi = W_COLS[name]
            return w_sb[:, k, lo + a:(hi if b is None else lo + b)]

        def v(name, i=0):
            c = V_COLS[name] + i
            return vec[:, c:c + 1]

        def mat(name):
            return mats[:, M_COL[name], :]

        h_sb = sb("h_sb", [P, HALVES, GB, KEYS])
        xa_sb = sb("xa_sb", [P, HALVES, T])
        mask_i = sb("mask_i", [P, GB, S], i32)
        mask_b = sb("mask_b", [P, GB, S], bf16)
        qt = sb("qt", [P, HALVES, GB, 2, S])
        kt = sb("kt", [P, HALVES, GB, KEYS])
        vv = sb("vv", [P, GB, C])
        neg_max = sb("neg_max", [P, 2, 4])
        sums = sb("sums", [P, 2, 4])
        rsum = sb("rsum", [P, 2, 4])
        probs = sb("probs", [P, 3, 4, KEYS])
        probs_t = sb("probs_t", [P, 2, 4, P])
        o_even = sb("o_even", [P, 4, S])
        attn = sb("attn", [P, GB, HALVES, S])
        y = sb("y", [P, HALVES, T])
        ysq = sb("ysq", [P, HALVES, T])
        a_ms = sb("a_ms", [P, T])
        hid = sb("hid", [P, 2, 2, T])
        x1 = sb("x1", [P, HALVES, T])

        st_sb = sb("st_sb", [P, 2, HALVES, GB])
        s0_sb = sb("s0_sb", [P, RH, HALVES, GB])
        xc = sb("xc", [P, HALVES, T])
        sq = sb("sq", [P, HALVES, T])
        r_ms = sb("r_ms", [P, T])
        xs = sb("xs", [P, HALVES, GB, S + 1])
        sx = sb("sx", [P, HALVES, T])
        z = sb("z", [P, HALVES, T])
        th = sb("th", [P, 2, T])
        tmp = sb("tmp", [P, 2, HALVES, T])
        xm = sb("xm", [P, 2, HALVES, T])
        tw = sb("tw", [P, T])
        e1 = sb("e1", [P, HALVES, T])
        decay = sb("decay", [P, HALVES, GB, S])
        rr = sb("rr", [P, HALVES, T])
        kk = sb("kk", [P, HALVES, T])
        vr = sb("vr", [P, HALVES, T])
        gt = sb("gt", [P, HALVES, T])
        gate = sb("gate", [P, HALVES, T])
        kv = sb("kv", [P, RH, HALVES * GB, S])
        vb = sb("vb", [P, RH, HALVES * T])
        st = sb("st", [P, 2, HALVES * T])
        rs = sb("rs", [P, 4, HALVES * T])
        rk = sb("rk", [P, HALVES, T])
        bonus = sb("bonus", [P, HALVES, T])
        og = sb("og", [P, HALVES, T])
        gsq = sb("gsq", [P, HALVES, T])
        g_ms = sb("g_ms", [P, HALVES, T])
        x2 = sb("x2", [P, HALVES, T])
        relu = sb("relu", [P, HALVES, T])
        act = sb("act", [P, HALVES, T])
        tr = sb("tr", [P, HALVES, T])
        ft = sb("ft", [P, HALVES, T])

        psum = [ctx.enter_context(nc.psum_tensor(f"bank{i}", [P, 512], fp32)) for i in range(8)]
        A_BANK, R_BANK = psum[0:2], psum[4:7]
        pt_ps, o_ps, red_ps = psum[2], psum[3], psum[7]

        def flat(t):
            return t[:, :, :].rearrange("p h t -> p (h t)")

        def by_batch(ap):
            return ap.rearrange("p (b s) -> p b s", b=GB)

        def by_half(ap):
            return ap[:, :].rearrange("p (h t) -> p h t", h=HALVES)

        def batches(ap):
            return ap.rearrange("p (b s) -> p b s", s=S)

        def both(ap):
            return ap.unsqueeze(1).broadcast_to([P, HALVES, T])

        def vr_rows(j):
            return flat(vr)[j:P:RH, :].unsqueeze(1).broadcast_to([P // RH, RH, HALVES * T])

        ld_vec, ld_mats, ld_w2, ld_small = (Event(n, 0) for n in ("vec_in", "mats_in", "w2_in", "small_in"))
        ld_w = [Event(f"weights_in{i}", 0) for i in range(3)]
        fills, folded, bias_sum = Event("fills", 0), Event("folded", 0), Event("bias_sum", 0)
        h_in, xa_in, mask_in, st_in, s0_in = (Event(n, 16) for n in ("h_in", "xa_in", "mask_in", "st_in", "s0_in"))
        out_done = Event("out_done", 16)
        a_full = [Event(f"a_full{i}", A_USES[i]) for i in range(2)]
        a_free = [Event(f"a_free{i}", A_USES[i]) for i in range(2)]
        r_full = [Event(f"r_full{i}", R_USES[i]) for i in range(3)]
        r_free = [Event(f"r_free{i}", R_USES[i]) for i in range(3)]
        pt_full, pt_free = Event("pt_full", UNITS), Event("pt_free", UNITS)
        o_full, o_free = Event("o_full", BPS + 1), Event("o_free", BPS + 1)
        red_full = Event("red_full", 1)
        mask_made = Event("mask_made", 1)
        max_made, rsum_made, norm_made = (Event(n, UNITS) for n in ("max_made", "rsum_made", "norm_made"))
        o_even_made = Event("o_even_made", BPS)
        ysq_made, arstd_made, yn_made = (Event(n, 1) for n in ("ysq_made", "arstd_made", "yn_made"))
        sq_made, rstd_made, xn_made = (Event(n, 2) for n in ("sq_made", "rstd_made", "xn_made"))
        xs_made, row_made, sx_made = (Event(n, 2) for n in ("xs_made", "row_made", "sx_made"))
        z_made, xm_made = Event("z_made", 1), Event("xm_made", MIX)
        decay_made, gt_made = Event("decay_made", 1), Event("gt_made", 1)
        first_made, kv_made, st_made, rs_made = Event("first_made", 1), Event("kv_made", RH), Event("st_made", RH), Event("rs_made", RH)
        gathered = Event("gathered", RH)
        vb_in = [Event(f"vb_in{j}", 16) for j in range(RH)]
        rk_made = Event("rk_made", 1)
        gate_made, gate_b_made, gsq_made, gated = (Event(n, 1) for n in ("gate_made", "gate_b_made", "gsq_made", "gated"))
        grstd_made, og_scaled, og_made = (Event(n, 1) for n in ("grstd_made", "og_scaled", "og_made"))
        shift_made, act_made, fin_made = Event("shift_made", 2), Event("act_made", 1), Event("fin_made", 1)

        def a_bank(*name):
            return A_BANK[A_SLOT[name][0]]

        def a_open(g, *name):
            b, use = A_SLOT[name]
            return a_free[b].sem, count(a_free[b], g, use)

        def a_ready(g, *name):
            b, use = A_SLOT[name]
            return a_full[b].sem, count(a_full[b], g, use + 1)

        def a_taken(g, *name):
            b, use = A_SLOT[name]
            return a_free[b].sem, count(a_free[b], g, use + 1)

        def a_filled(*name):
            return a_full[A_SLOT[name][0]].sem

        def a_read(*name):
            return a_free[A_SLOT[name][0]].sem

        def r_bank(*name):
            return R_BANK[R_SLOT[name][0]]

        def r_open(g, *name):
            b, use = R_SLOT[name]
            return r_free[b].sem, count(r_free[b], g, use)

        def r_ready(g, *name):
            b, use = R_SLOT[name]
            return r_full[b].sem, count(r_full[b], g, use + 1)

        def r_taken(g, *name):
            b, use = R_SLOT[name]
            return r_free[b].sem, count(r_free[b], g, use + 1)

        def r_filled(*name):
            return r_full[R_SLOT[name][0]].sem

        def r_read(*name):
            return r_free[R_SLOT[name][0]].sem

        def run(eng, attention, recurrent):
            def turn(i, streams="ANR"):
                for stream, piece in TURN:
                    if stream not in streams:
                        continue
                    if stream == "A":
                        attention(i, piece)
                    elif stream == "N":
                        attention(i + 1, piece)
                    else:
                        recurrent(i - 1, piece)

            for stream, piece in TURN:
                if stream == "N":
                    attention(FIRST, piece)
            turn(0, "AN")
            turn(1)
            with eng.Fori(2, GROUPS - 1) as i:
                turn(i)
            turn(GROUPS - 1, "AR")
            turn(GROUPS, "R")

        block = ctx.enter_context(nc.Block())

        @block.sync
        def _(sp):
            def load_attention(g):
                b, use = A_SLOT[("v", 1)]
                sp.wait_ge(a_full[b].sem, count(a_full[b], g - 1, use + 1))
                sp.dma_start(h_sb[:, :, :, :], hT[g, :, :, :, :]).then_inc(h_in.sem, 16)
                sp.wait_ge(mask_made.sem, count(mask_made, g, 0))
                sp.dma_start(mask_i[:, :, :].rearrange("p b s -> p (b s)"), maskT[g, :].partition_broadcast(P)).then_inc(mask_in.sem, 16)

            def load_residual(g):
                sp.wait_ge(o_free.sem, count(o_free, g, 0))
                sp.dma_start(xa_sb[:, :, :], xT[g, :, :, :]).then_inc(xa_in.sem, 16)

            def load_state(g):
                sp.wait_ge(row_made.sem, count(row_made, g, 0))
                sp.dma_start(st_sb[:, :, :, :], stT[g, :, :, :, :]).then_inc(st_in.sem, 16)
                sp.wait_ge(first_made.sem, count(first_made, g, 0))
                sp.dma_start(s0_sb[:, :, :, :], s0T[g, :, :, :, :]).then_inc(s0_in.sem, 16)

            def spread(g):
                sp.wait_ge(*r_taken(g, "V"))
                for j in range(RH):
                    sp.dma_start(vb[:, j, :], vr_rows(j)).then_inc(vb_in[j].sem, 16)

            def store(g):
                sp.wait_ge(fin_made.sem, count(fin_made, g, 1))
                sp.dma_start(out[g, :, :, :], x2[:, :, :]).then_inc(out_done.sem, 16)

            def load_weights(n):
                lo, hi = W_COLS[W_PARTS[n][0]][0], W_COLS[W_PARTS[n][1]][1]
                sp.dma_start(w_sb[:, :, lo:hi], W[:, :, lo:hi]).then_inc(ld_w[n].sem, 16)

            sp.dma_start(vec[:, :], VEC[:, :]).then_inc(ld_vec.sem, 16)
            load_weights(0)
            load_attention(0)
            sp.dma_start(mats[:, :, :], MATS[:, :, :]).then_inc(ld_mats.sem, 16)
            load_weights(1)
            load_residual(0)
            sp.dma_start(w2_sb[:, :, :], W2[:, :, :]).then_inc(ld_w2.sem, 16)
            load_weights(2)
            sp.dma_start(maa2_sb[:, :, :], MAA2[:, :, :]).then_inc(ld_small.sem, 16)
            sp.dma_start(td2_sb[:, :], TD2[:, :]).then_inc(ld_small.sem, 16)
            load_attention(1)
            load_state(0)
            load_residual(1)

            def turn(i):
                store_before = i - 2
                if not (isinstance(i, int) and store_before < 0):
                    store(store_before)
                if not (isinstance(i, int) and i + 1 >= GROUPS):
                    load_attention(i + 1)
                spread(i - 1)
                load_state(i)
                if not (isinstance(i, int) and i + 1 >= GROUPS):
                    load_residual(i + 1)

            turn(1)
            turn(2)
            with sp.Fori(3, GROUPS - 1) as i:
                turn(i)
            turn(GROUPS - 1)
            store(GROUPS - 2)
            spread(GROUPS - 1)
            store(GROUPS - 1)
            sp.wait_ge(out_done.sem, 16 * GROUPS)

        @block.tensor
        def _(pe):
            mm = nc.tensor.matmul

            def project(bank, name, rhs, blocks=(0, 1), widths=(P, P)):
                for n, (m, width) in enumerate(zip(blocks, widths)):
                    for k in range(HALVES):
                        last = mm(bank[0:width, n * T:(n + 1) * T], w(name, k, m * P, m * P + width), rhs[k], start=(k == 0), stop=(k == 1))
                return last

            def average(bank, src):
                mm(bank[:, 0:T], mat("mean256"), src[:, 0, :], start=True, stop=False)
                return mm(bank[:, 0:T], mat("mean256"), src[:, 1, :], start=False, stop=True)

            def scores(g, u):
                bp, r = unit(u)
                bank = a_bank("s", u)
                pe.wait_ge(*a_open(g, "s", u))
                rows = slice(32 * r, 32 * r + 32)
                for n in range(4):
                    b, h = 2 * bp + n // 2, n % 2
                    mm(bank[:, n * P:(n + 1) * P], qt[rows, h, b, :, :].rearrange("p e s -> p (e s)"), kt[rows, h, b, :],
                       start=(n == 0), stop=False, skip_group_check=True)
                row = slice(32 * r, 32 * r + 1)
                for n in range(4):
                    last = mm(bank[:, n * P:n * P + S], ones_bf[row, :], mask_b[row, 2 * bp + n // 2, :],
                              start=False, stop=True, skip_group_check=True)
                last.then_inc(a_filled("s", u), 1)

            def transpose(g, u):
                pe.wait_ge(norm_made.sem, count(norm_made, g, u + 1))
                pe.wait_ge(pt_free.sem, count(pt_free, g, u))
                for n in range(4):
                    last = nc.tensor.transpose(pt_ps[:, n * P:(n + 1) * P], probs[:, PROBS(u), n, :], mat("ident"))
                last.then_inc(pt_full.sem, 1)

            def values(g, u):
                bp, r = unit(u)
                pe.wait_ge(pt_free.sem, count(pt_free, g, u + 1))
                if r == 0:
                    pe.wait_ge(o_free.sem, count(o_free, g, bp))
                for n in range(4):
                    b, h = 2 * bp + n // 2, n % 2
                    last = mm(o_ps[32 * r:32 * r + 32, n * P:(n + 1) * P], vv[:, b, h * P + 32 * r:h * P + 32 * r + 32],
                              probs_t[:, u % 2, n, :], start=True, stop=True)
                if r == PAIRS - 1:
                    last.then_inc(o_full.sem, 1)

            def attention(g, piece):
                if piece == "q":
                    if g is FIRST:
                        pe.wait_ge(ld_w[0].sem, 16)
                    pe.wait_ge(h_in.sem, count(h_in, g, 16))
                    pe.wait_ge(*a_open(g, "q"))
                    project(a_bank("q"), "q", [h_sb[:, k, :, S:KEYS] for k in range(HALVES)]).then_inc(a_filled("q"), 1)
                elif piece == "k":
                    for m in range(2):
                        pe.wait_ge(*a_open(g, "k", m))
                        for k in range(HALVES):
                            last = mm(a_bank("k", m)[:, :], w("k", k, m * P, m * P + P), h_sb[:, k, :, :], start=(k == 0), stop=(k == 1))
                        last.then_inc(a_filled("k", m), 1)
                elif piece[0] == "v":
                    n = int(piece[1])
                    bank = a_bank("v", n)
                    pe.wait_ge(*a_open(g, "v", n))
                    for i in range(2):
                        for k in range(HALVES):
                            last = mm(bank[:, i * C:(i + 1) * C], h_sb[:, k, 2 * n + i, :], w("v", k), start=(k == 0), stop=(k == 1))
                    last.then_inc(a_filled("v", n), 1)
                    if g is FIRST and n == 1:
                        pe.wait_ge(ld_mats.sem, 16)
                        pe.wait_ge(fills.sem, FILLS)
                        pe.wait_ge(ld_w[1].sem, 16)
                        for m in range(2):
                            for k in range(2):
                                last = mm(red_ps[:, m:m + 1], w("o", k, m * P, m * P + P), v("v_b", k), start=(k == 0), stop=(k == 1))
                        last.then_inc(bias_sum.sem, 1)
                elif piece[0] == "u":
                    s = int(piece[1:])
                    if s == 0:
                        pe.wait_ge(mask_made.sem, count(mask_made, g, 1))
                        for n in range(2):
                            pe.wait_ge(*a_taken(g, "k", n))
                    if s < UNITS:
                        scores(g, s)
                    if 2 <= s <= UNITS + 1:
                        transpose(g, s - 2)
                    if s == 3:
                        for n in range(2):
                            pe.wait_ge(*a_taken(g, "v", n))
                    if s >= 3:
                        values(g, s - 3)
                elif piece == "o":
                    pe.wait_ge(o_free.sem, count(o_free, g, BPS))
                    pe.wait_ge(*a_open(g, "o"))
                    project(a_bank("o"), "o", [attn[:, :, k, :] for k in range(HALVES)]).then_inc(a_filled("o"), 1)
                elif piece == "rms":
                    pe.wait_ge(ysq_made.sem, count(ysq_made, g, 1))
                    pe.wait_ge(*a_open(g, "rms"))
                    average(a_bank("rms"), ysq).then_inc(a_filled("rms"), 1)
                elif piece[0:3] == "mlp":
                    n = int(piece[3])
                    if n == 0:
                        if g is FIRST:
                            pe.wait_ge(folded.sem, FOLDS)
                            pe.wait_ge(ld_w2.sem, 16)
                        pe.wait_ge(yn_made.sem, count(yn_made, g, 1))
                    pe.wait_ge(*a_open(g, "w1", n))
                    project(a_bank("w1", n), "w1", [y[:, k, :] for k in range(HALVES)], (2 * n, 2 * n + 1)).then_inc(a_filled("w1", n), 1)
                    if n >= 1:
                        contract(g, n - 1)
                elif piece == "x1":
                    contract(g, FM // 2 - 1).then_inc(o_full.sem, 1)

            def contract(g, n):
                pe.wait_ge(*a_taken(g, "w1", n))
                for i in range(2):
                    for m in range(HALVES):
                        last = mm(o_ps[:, m * T:(m + 1) * T], w2_sb[:, 2 * n + i, m * P:(m + 1) * P], hid[:, n % 2, i, :],
                                  start=(n == 0 and i == 0 and m == 0), stop=(n == FM // 2 - 1 and i == 1), skip_group_check=True)
                return last

            def gather(g, j):
                if j == 0:
                    pe.wait_ge(gated.sem, count(gated, g, 0))
                pe.wait_ge(rs_made.sem, count(rs_made, g, j + 1))
                mm(red_ps[:, :], mat(f"gather{j}"), rs[:, j % 4, :], start=(j == 0), stop=False).then_inc(gathered.sem, 1)

            def recurrent(g, piece):
                if piece in ("mean0", "mean1"):
                    n = int(piece[-1])
                    if n == 0:
                        pe.wait_ge(o_free.sem, count(o_free, g, BPS + 1))
                    else:
                        pe.wait_ge(*r_taken(g, "O"))
                    pe.wait_ge(*r_open(g, "mean", n))
                    average(r_bank("mean", n), (x1, x2)[n]).then_inc(r_filled("mean", n), 1)
                elif piece in ("var0", "var1"):
                    n = int(piece[-1])
                    pe.wait_ge(sq_made.sem, count(sq_made, g, n + 1))
                    pe.wait_ge(*r_open(g, "var", n))
                    average(r_bank("var", n), sq).then_inc(r_filled("var", n), 1)
                elif piece == "maa":
                    pe.wait_ge(ld_w[2].sem, 16)
                    pe.wait_ge(ld_small.sem, 32)
                    pe.wait_ge(z_made.sem, count(z_made, g, 1))
                    pe.wait_ge(*r_open(g, "maa"))
                    project(r_bank("maa"), "maa1", [z[:, k, :] for k in range(HALVES)], (0, 1), (P, DM)).then_inc(r_filled("maa"), 1)
                elif piece[0] == "x":
                    n = int(piece[1])
                    if n == 0:
                        pe.wait_ge(*r_taken(g, "maa"))
                    bank = r_bank("x", n)
                    pe.wait_ge(*r_open(g, "x", n))
                    for m in range(HALVES):
                        last = mm(bank[:, m * T:(m + 1) * T], maa2_sb[:, ORDER[n], m * P:(m + 1) * P], th[:, ORDER[n] // 4, :], start=True, stop=True)
                    last.then_inc(r_filled("x", n), 1)
                    shifted = [xm[:, (n - 1) % 2, k, :] for k in range(HALVES)]
                    if n >= 1:
                        pe.wait_ge(xm_made.sem, count(xm_made, g, n))
                    if n == 1:
                        pe.wait_ge(*r_open(g, "td1"))
                        project(r_bank("td1"), "td1", shifted, (0,), (DD,)).then_inc(r_filled("td1"), 1)
                    if n == 2:
                        pe.wait_ge(*r_taken(g, "td1"))
                        pe.wait_ge(*r_open(g, "td2"))
                        for m in range(HALVES):
                            last = mm(r_bank("td2")[:, m * T:(m + 1) * T], td2_sb[:, m * P:(m + 1) * P], tw[:, :], start=True, stop=True)
                        last.then_inc(r_filled("td2"), 1)
                    if n >= 2:
                        to = {2: "K", 3: "V", 4: "R"}[n]
                        pe.wait_ge(*r_open(g, to))
                        project(r_bank(to), "W" + to.lower(), shifted).then_inc(r_filled(to), 1)
                elif piece == "G":
                    pe.wait_ge(xm_made.sem, count(xm_made, g, MIX))
                    pe.wait_ge(*r_open(g, "G"))
                    project(r_bank("G"), "Wg", [xm[:, (MIX - 1) % 2, k, :] for k in range(HALVES)]).then_inc(r_filled("G"), 1)
                elif piece[0] == "s":
                    j = int(piece[1])
                    if j == RH:
                        pe.wait_ge(rk_made.sem, count(rk_made, g, 1))
                        pe.wait_ge(*r_open(g, "coef"))
                        for m in range(HALVES):
                            last = mm(r_bank("coef")[:, m * T:(m + 1) * T], bonus_w[:, m, :], rk[:, m, :], start=True, stop=True)
                        last.then_inc(r_filled("coef"), 1)
                    if j >= 2:
                        gather(g, j - 2)
                    if j == RH + 1:
                        pe.wait_ge(*r_taken(g, "coef"))
                        mm(red_ps[:, :], mat("center8"), flat(bonus), start=False, stop=True).then_inc(red_full.sem, 1)
                elif piece == "gn":
                    pe.wait_ge(gsq_made.sem, count(gsq_made, g, 1))
                    pe.wait_ge(*r_open(g, "gvar"))
                    mm(r_bank("gvar")[:, :], mat("mean8"), flat(gsq), start=True, stop=True).then_inc(r_filled("gvar"), 1)
                elif piece == "O":
                    pe.wait_ge(og_made.sem, count(og_made, g, 1))
                    pe.wait_ge(*r_open(g, "O"))
                    project(r_bank("O"), "Wo", [og[:, k, :] for k in range(HALVES)]).then_inc(r_filled("O"), 1)
                elif piece in ("fk", "fr"):
                    n = ("fk", "fr").index(piece)
                    pe.wait_ge(shift_made.sem, count(shift_made, g, n + 1))
                    pe.wait_ge(*r_open(g, piece))
                    project(r_bank(piece), "W" + piece, [xm[:, n, k, :] for k in range(HALVES)]).then_inc(r_filled(piece), 1)
                elif piece == "fv":
                    pe.wait_ge(act_made.sem, count(act_made, g, 1))
                    pe.wait_ge(*r_open(g, "fv"))
                    project(r_bank("fv"), "Wfv", [act[:, k, :] for k in range(HALVES)]).then_inc(r_filled("fv"), 1)

            run(pe, attention, recurrent)

        @block.scalar
        def _(sc):
            fn = nc.scalar.activation

            def attention(g, piece):
                if piece == "k":
                    if g is FIRST:
                        sc.wait_ge(ld_vec.sem, 16)
                    for m in range(2):
                        sc.wait_ge(*a_ready(g, "k", m))
                        fn(kt[:, m, :, :].rearrange("p b s -> p (b s)"), a_bank("k", m)[:, :], ACT.Identity, bias=v("k_b", m)).then_inc(a_read("k", m), 1)
                elif piece[0] == "v":
                    n = int(piece[1])
                    sc.wait_ge(*a_ready(g, "v", n))
                    fn(vv[:, 2 * n:2 * n + 2, :].rearrange("p b s -> p (b s)"), a_bank("v", n)[:, :], ACT.Copy).then_inc(a_read("v", n), 1)
                elif piece[0] == "u":
                    s = int(piece[1:])
                    if s < UNITS:
                        sc.wait_ge(max_made.sem, count(max_made, g, s + 1))
                        sc.wait_ge(norm_made.sem, count(norm_made, g, max(s - 1, 0)))
                        sc.wait_ge(pt_full.sem, count(pt_full, g, max(s - 2, 0)))
                        bank = a_bank("s", s)
                        for n in range(4):
                            last = fn(probs[:, PROBS(s), n, :], bank[:, n * P:(n + 1) * P], ACT.Exp,
                                      bias=neg_max[:, s % 2, n:n + 1], accum_out=sums[:, s % 2, n:n + 1])
                        last.then_inc(a_read("s", s), 1)
                    if s >= 6 and (s - 6) % 4 == 0:
                        bp = (s - 6) // 4
                        sc.wait_ge(o_full.sem, count(o_full, g, bp + 1))
                        sc.wait_ge(o_free.sem, count(o_free, g, bp))
                        fn(o_even[:, :, :], o_ps[:, :].rearrange("p (n e s) -> p n e s", n=4, e=2)[:, :, 0, :], ACT.Copy,
                           scale=v("even")).then_inc(o_even_made.sem, 1)
                elif piece == "o":
                    sc.wait_ge(*a_taken(g, "o"))
                    fn(ysq[:, :, :], y[:, :, :], ACT.Square).then_inc(ysq_made.sem, 1)
                elif piece == "rms":
                    sc.wait_ge(*a_ready(g, "rms"))
                    fn(a_ms[:, :], a_bank("rms")[:, 0:T], ACT.Sqrt, bias=v("eps6")).then_inc(a_read("rms"), 1)
                elif piece[0:3] == "mlp":
                    n = int(piece[3])
                    sc.wait_ge(*a_ready(g, "w1", n))
                    for i in range(2):
                        last = fn(hid[:, n % 2, i, :], a_bank("w1", n)[:, i * T:(i + 1) * T], ACT.Gelu_apprx_tanh, bias=v("b1", 2 * n + i))
                    last.then_inc(a_read("w1", n), 1)

            def recurrent(g, piece):
                if piece in ("mean0", "mean1"):
                    n = int(piece[-1])
                    sc.wait_ge(*r_taken(g, "mean", n))
                    fn(sq[:, :, :], xc[:, :, :], ACT.Square).then_inc(sq_made.sem, 1)
                    sc.wait_ge(st_in.sem, count(st_in, g, 16))
                    sc.wait_ge(sx_made.sem, count(sx_made, g, n))
                    fn(xs[:, :, :, 0], st_sb[:, 1 - n, :, :], ACT.Copy).then_inc(row_made.sem, 1)
                elif piece in ("var0", "var1"):
                    n = int(piece[-1])
                    sc.wait_ge(*r_ready(g, "var", n))
                    fn(r_ms[:, :], r_bank("var", n)[:, 0:T], ACT.Sqrt, bias=v("eps5")).then_inc(r_read("var", n), 1)
                elif piece == "maa":
                    sc.wait_ge(*r_ready(g, "maa"))
                    fn(th[:, 0, :], r_bank("maa")[:, 0:T], ACT.Tanh)
                    fn(th[0:DM, 1, :], r_bank("maa")[0:DM, T:2 * T], ACT.Tanh).then_inc(r_read("maa"), 1)
                elif piece == "x1":
                    sc.wait_ge(*r_ready(g, "td1"))
                    fn(tw[0:DD, :], r_bank("td1")[0:DD, 0:T], ACT.Tanh).then_inc(r_read("td1"), 1)
                elif piece == "x2":
                    sc.wait_ge(*r_ready(g, "td2"))
                    for m in range(HALVES):
                        last = fn(e1[:, m, :], r_bank("td2")[:, m * T:(m + 1) * T], ACT.Exp, bias=v("td", m))
                    last.then_inc(r_read("td2"), 1)
                    copy(g, "K", kk)
                    sc.wait_ge(*r_taken(g, "td2"))
                    fn(decay[:, :, :, :].rearrange("p h b s -> p (h b) s")[:, :, 1:S], batches(flat(e1))[:, :, 0:S - 1],
                       ACT.Exp, scale=-1.0).then_inc(decay_made.sem, 1)
                elif piece == "x3":
                    sc.wait_ge(s0_in.sem, count(s0_in, g, 16))
                    sc.wait_ge(st_made.sem, count(st_made, g, 0))
                    fn(kv[:, :, :, 0], s0_sb[:, :, :, :].rearrange("p j h b -> p j (h b)"), ACT.Copy).then_inc(first_made.sem, 1)
                    copy(g, "V", vr)
                elif piece == "x4":
                    copy(g, "R", rr)
                elif piece == "G":
                    sc.wait_ge(*r_ready(g, "G"))
                    fn(flat(gt), r_bank("G")[:, :], ACT.Tanh, scale=0.5).then_inc(gt_made.sem, 1)
                elif piece == "s9":
                    sc.wait_ge(red_full.sem, count(red_full, g, 1))
                    fn(flat(gsq), red_ps[:, :], ACT.Square).then_inc(gsq_made.sem, 1)
                elif piece == "gn":
                    sc.wait_ge(*r_ready(g, "gvar"))
                    fn(flat(g_ms), r_bank("gvar")[:, :], ACT.Sqrt, bias=v("eps5")).then_inc(r_read("gvar"), 1)
                elif piece == "fk":
                    sc.wait_ge(*r_ready(g, "fk"))
                    fn(flat(relu), r_bank("fk")[:, :], ACT.Relu).then_inc(r_read("fk"), 1)
                elif piece == "fr":
                    sc.wait_ge(*r_ready(g, "fr"))
                    fn(flat(tr), r_bank("fr")[:, :], ACT.Tanh, scale=0.5).then_inc(r_read("fr"), 1)

            def copy(g, name, to):
                sc.wait_ge(*r_ready(g, name))
                fn(flat(to), r_bank(name)[:, :], ACT.Copy).then_inc(r_read(name), 1)

            run(sc, attention, recurrent)

        @block.vector
        def _(ve):
            tt, ts, stt, invert = nc.vector.tensor_tensor, nc.vector.tensor_scalar, nc.vector.scalar_tensor_tensor, nc.vector.reciprocal

            def shift(to, name, event):
                for h in range(HALVES):
                    last = stt(by_batch(to[:, h, :]), by_batch(sx[:, h, :]), v(name, h), xs[:, h, :, 1:S + 1], ALU.mult, ALU.add)
                last.then_inc(event.sem, 1)

            def attention(g, piece):
                if piece == "q":
                    if g is FIRST:
                        ve.wait_ge(ld_vec.sem, 16)
                        for e, name in enumerate(("even16", "odd16")):
                            ts(q_bias[:, e, :], vec[:, V_COLS["q_b"]:V_COLS["q_b"] + 2], v(name), None, ALU.mult).then_inc(folded.sem, 1)
                        ve.wait_ge(folded.sem, 2)
                    ve.wait_ge(mask_in.sem, count(mask_in, g, 16))
                    ts(mask_b[:, :, :], mask_i[:, :, :], 0, NEG, ALU.is_equal, ALU.mult).then_inc(mask_made.sem, 1)
                    ve.wait_ge(*a_ready(g, "q"))
                    for m in range(HALVES):
                        for e, name in enumerate(("even16", "odd16")):
                            last = ts(qt[:, m, :, e, :], by_batch(a_bank("q")[:, m * T:(m + 1) * T]), v(name), q_bias[:, e, m:m + 1], ALU.mult, ALU.add)
                    last.then_inc(a_read("q"), 1)
                elif piece == "v1":
                    if g is FIRST:
                        ve.wait_ge(ld_w[1].sem, 16)
                        for k in range(2):
                            ts(w("w1", k), w("w1", k), v("pn", k), None, ALU.mult).then_inc(folded.sem, 1)
                        ve.wait_ge(bias_sum.sem, 1)
                        tt(o_bias[:, :], red_ps[:, 0:2], vec[:, V_COLS["o_b"]:V_COLS["o_b"] + 2], ALU.add).then_inc(folded.sem, 1)
                        ve.wait_ge(ld_mats.sem, 16)
                        for k in range(2):
                            ts(bonus_w[:, k, :], mat("same_head"), v("u", k), None, ALU.mult).then_inc(folded.sem, 1)
                elif piece[0] == "u":
                    s = int(piece[1:])
                    if 1 <= s <= UNITS:
                        ve.wait_ge(*a_taken(g, "s", s - 1))
                        invert(rsum[:, (s - 1) % 2, :], sums[:, (s - 1) % 2, :]).then_inc(rsum_made.sem, 1)
                    if s < UNITS:
                        ve.wait_ge(*a_ready(g, "s", s))
                        nc.vector.tensor_reduce(neg_max[:, s % 2, :], a_bank("s", s)[:, :].rearrange("p (n k) -> p n k", n=4), AX.X, ALU.max,
                                                negate=True).then_inc(max_made.sem, 1)
                    if 2 <= s <= UNITS + 1:
                        ve.wait_ge(pt_full.sem, count(pt_full, g, s - 1))
                        nc.vector.tensor_copy(probs_t[:, s % 2, :, :].rearrange("p n q -> p (n q)"), pt_ps[:, :]).then_inc(pt_free.sem, 1)
                    if s >= 6 and (s - 6) % 4 == 0:
                        bp = (s - 6) // 4
                        ve.wait_ge(o_even_made.sem, count(o_even_made, g, bp + 1))
                        stt(attn[:, 2 * bp:2 * bp + 2, :, :].rearrange("p b h s -> p (b h) s"),
                            o_ps[:, :].rearrange("p (n e s) -> p n e s", n=4, e=2)[:, :, 1, :], v("odd"), o_even[:, :, :],
                            ALU.mult, ALU.add).then_inc(o_free.sem, 1)
                    if g is FIRST and s == 4:
                        ve.wait_ge(ld_w[2].sem, 16)
                        for name in ("Wo", "Wfv"):
                            for k in range(2):
                                ts(w(name, k), w(name, k), 0.5, None, ALU.mult).then_inc(folded.sem, 1)
                        ve.wait_ge(folded.sem, FOLDS)
                elif piece == "o":
                    ve.wait_ge(xa_in.sem, count(xa_in, g, 16))
                    ve.wait_ge(*a_ready(g, "o"))
                    for m in range(HALVES):
                        last = stt(y[:, m, :], a_bank("o")[:, m * T:(m + 1) * T], o_bias[:, m:m + 1], xa_sb[:, m, :], ALU.add, ALU.add)
                    last.then_inc(a_read("o"), 1)
                elif piece == "rms":
                    ve.wait_ge(*a_taken(g, "rms"))
                    invert(a_ms[:, :], a_ms[:, :]).then_inc(arstd_made.sem, 1)
                    ve.wait_ge(arstd_made.sem, count(arstd_made, g, 1))
                    tt(y[:, :, :], y[:, :, :], both(a_ms[:, :]), ALU.mult).then_inc(yn_made.sem, 1)
                elif piece == "x1":
                    ve.wait_ge(*r_taken(g - 1, "O"))
                    ve.wait_ge(o_full.sem, count(o_full, g, BPS + 1))
                    for m in range(HALVES):
                        last = stt(x1[:, m, :], o_ps[:, m * T:(m + 1) * T], v("b2", m), xa_sb[:, m, :], ALU.add, ALU.add)
                    last.then_inc(o_free.sem, 1)

            def recurrent(g, piece):
                if piece in ("mean0", "mean1"):
                    n = int(piece[-1])
                    ve.wait_ge(*r_ready(g, "mean", n))
                    tt(xc[:, :, :], (x1, x2)[n][:, :, :], both(r_bank("mean", n)[:, 0:T]), ALU.subtract).then_inc(r_read("mean", n), 1)
                elif piece in ("norm0", "norm1"):
                    n = int(piece[-1])
                    ve.wait_ge(*r_taken(g, "var", n))
                    invert(r_ms[:, :], r_ms[:, :]).then_inc(rstd_made.sem, 1)
                    ve.wait_ge(rstd_made.sem, count(rstd_made, g, n + 1))
                    tt(xc[:, :, :], xc[:, :, :], both(r_ms[:, :]), ALU.mult).then_inc(xn_made.sem, 1)
                    ve.wait_ge(xn_made.sem, count(xn_made, g, n + 1))
                    name = ("ln1", "ln2")[n]
                    for h in range(HALVES):
                        last = ts(xs[:, h, :, 1:S + 1], by_batch(xc[:, h, :]), v(name + "_w", h), v(name + "_b", h), ALU.mult, ALU.add)
                    last.then_inc(xs_made.sem, 1)
                    ve.wait_ge(xs_made.sem, count(xs_made, g, n + 1))
                    ve.wait_ge(row_made.sem, count(row_made, g, n + 1))
                    rows = xs[:, :, :, :].rearrange("p h b s -> p (h b) s")
                    tt(batches(flat(sx)), rows[:, :, 0:S], rows[:, :, 1:S + 1], ALU.subtract).then_inc(sx_made.sem, 1)
                    ve.wait_ge(sx_made.sem, count(sx_made, g, n + 1))
                    if n == 0:
                        shift(z, "maa_x", z_made)
                    else:
                        shift(xm[:, 0, :, :], "fk", shift_made)
                        shift(xm[:, 1, :, :], "fr", shift_made)
                elif piece[0] == "x":
                    n = int(piece[1])
                    ve.wait_ge(*r_ready(g, "x", n))
                    ve.wait_ge(xm_made.sem, count(xm_made, g, max(0, n - 1)))
                    for h in range(HALVES):
                        last = stt(tmp[:, n % 2, h, :], r_bank("x", n)[:, h * T:(h + 1) * T], v("maa", 2 * ORDER[n] + h), sx[:, h, :], ALU.add, ALU.mult)
                    last.then_inc(r_read("x", n), 1)
                elif piece == "G":
                    ve.wait_ge(gt_made.sem, count(gt_made, g, 1))
                    stt(flat(gate), flat(gt), 1.0, r_bank("G")[:, :], ALU.add, ALU.mult).then_inc(r_read("G"), 1)
                    ve.wait_ge(*r_taken(g, "G"))
                    for h in range(HALVES):
                        last = ts(gt[:, h, :], gate[:, h, :], v("gn_b", h), None, ALU.mult)
                    last.then_inc(gate_b_made.sem, 1)
                    for h in range(HALVES):
                        last = ts(gate[:, h, :], gate[:, h, :], v("gn_w", h), None, ALU.mult)
                    last.then_inc(gate_made.sem, 1)
                elif piece[0] == "s":
                    j = int(piece[1])
                    if j == 0:
                        ve.wait_ge(*r_taken(g, "K"))
                        ve.wait_ge(decay_made.sem, count(decay_made, g, 1))
                        ve.wait_ge(first_made.sem, count(first_made, g, 1))
                    if j < RH:
                        ve.wait_ge(vb_in[j].sem, count(vb_in[j], g, 16))
                        tt(kv[:, j, :, 1:S], batches(vb[:, j, :])[:, :, 0:S - 1], batches(flat(kk))[:, :, 0:S - 1],
                           ALU.mult).then_inc(kv_made.sem, 1)
                        ve.wait_ge(kv_made.sem, count(kv_made, g, j + 1))
                        ve.wait_ge(rs_made.sem, count(rs_made, g, max(0, j - 1)))
                        nc.vector.tensor_tensor_scan(st[:, j % 2, :], decay[:, :, :, :].rearrange("p h b s -> p (h b s)"),
                                                     kv[:, j, :, :].rearrange("p b s -> p (b s)"), 0.0, ALU.mult, ALU.add).then_inc(st_made.sem, 1)
                    if j == RH:
                        ve.wait_ge(*r_ready(g, "coef"))
                        tt(flat(bonus), r_bank("coef")[:, :], flat(vr), ALU.mult).then_inc(r_read("coef"), 1)
                elif piece == "gn":
                    ve.wait_ge(gate_made.sem, count(gate_made, g, 1))
                    ve.wait_ge(gsq_made.sem, count(gsq_made, g, 1))
                    tt(flat(og), red_ps[:, :], flat(gate), ALU.mult).then_inc(gated.sem, 1)
                    ve.wait_ge(*r_taken(g, "gvar"))
                    invert(flat(g_ms), flat(g_ms)).then_inc(grstd_made.sem, 1)
                    ve.wait_ge(grstd_made.sem, count(grstd_made, g, 1))
                    tt(flat(og), flat(og), flat(g_ms), ALU.mult).then_inc(og_scaled.sem, 1)
                    ve.wait_ge(og_scaled.sem, count(og_scaled, g, 1))
                    tt(flat(og), flat(og), flat(gt), ALU.add).then_inc(og_made.sem, 1)
                elif piece == "O":
                    ve.wait_ge(out_done.sem, count(out_done, g, 0))
                    ve.wait_ge(*r_ready(g, "O"))
                    tt(flat(x2), r_bank("O")[:, :], flat(x1), ALU.add).then_inc(r_read("O"), 1)
                elif piece == "fv":
                    ve.wait_ge(*r_ready(g, "fv"))
                    ve.wait_ge(*r_taken(g, "fr"))
                    stt(flat(ft), flat(tr), 1.0, r_bank("fv")[:, :], ALU.add, ALU.mult).then_inc(r_read("fv"), 1)

            run(ve, attention, recurrent)

        @block.gpsimd
        def _(po):
            tt = nc.gpsimd.tensor_tensor
            po.memset(ones_bf[:, :], 1.0).then_inc(fills.sem, 1)
            po.memset(th[:, 1, :], 0.0).then_inc(fills.sem, 1)
            po.memset(tw[:, :], 0.0).then_inc(fills.sem, 1)
            po.memset(decay[:, :, :, 0], 0.0).then_inc(fills.sem, 1)
            po.wait_ge(fills.sem, FILLS)

            def attention(g, piece):
                if piece[0] == "u":
                    u = int(piece[1:]) - 1
                    if 0 <= u < UNITS:
                        po.wait_ge(rsum_made.sem, count(rsum_made, g, u + 1))
                        tt(probs[:, PROBS(u), :, :], probs[:, PROBS(u), :, :], rsum[:, u % 2, :].unsqueeze(2).broadcast_to([P, 4, KEYS]),
                           ALU.mult).then_inc(norm_made.sem, 1)

            def recurrent(g, piece):
                if piece[0] == "x":
                    n = int(piece[1])
                    po.wait_ge(*r_taken(g, "x", n))
                    tt(xm[:, n % 2, :, :].rearrange("p h (b s) -> p (h b) s", b=GB), tmp[:, n % 2, :, :].rearrange("p h (b s) -> p (h b) s", b=GB),
                       xs[:, :, :, :].rearrange("p h b s -> p (h b) s")[:, :, 1:S + 1], ALU.add).then_inc(xm_made.sem, 1)
                elif piece[0] == "s":
                    j = int(piece[1])
                    if j == 0:
                        po.wait_ge(*r_taken(g, "K"))
                        po.wait_ge(*r_taken(g, "R"))
                        tt(flat(rk), flat(rr), flat(kk), ALU.mult).then_inc(rk_made.sem, 1)
                    if j < RH:
                        po.wait_ge(st_made.sem, count(st_made, g, j + 1))
                        po.wait_ge(gathered.sem, count(gathered, g, max(0, j - 3)))
                        tt(rs[:, j % 4, :], st[:, j % 2, :], flat(rr), ALU.mult).then_inc(rs_made.sem, 1)
                elif piece == "fk":
                    po.wait_ge(*r_taken(g, "fk"))
                    tt(flat(act), flat(relu), flat(relu), ALU.mult).then_inc(act_made.sem, 1)
                elif piece == "fv":
                    po.wait_ge(*r_taken(g, "fv"))
                    tt(flat(x2), flat(x2), flat(ft), ALU.add).then_inc(fin_made.sem, 1)

            run(po, attention, recurrent)


FILLS, FOLDS = 4, 11
BPS = GB // 2


def PROBS(u):
    return u % 3


def unit(u):
    return u // PAIRS, u % PAIRS


def kernel(**inputs):
    import numpy as np
    import concourse.bacc as bacc
    from concourse import mybir as my
    from concourse.bass_utils import run_bass_kernel_spmd

    a = {n: np.asarray(x) for n, x in inputs.items()}
    l0 = {n[len("L0_xattn_"):]: x for n, x in a.items() if n.startswith("L0_xattn_")}
    l1 = {n[len("L1_xattn_"):]: x for n, x in a.items() if n.startswith("L1_xattn_")}
    x, ctx = a["x"], a["ctx_2048"]

    def halves(m):
        return m.reshape(HALVES, P, -1).transpose(1, 0, 2)

    def grouped(z):
        return z.reshape(GROUPS, GB, z.shape[1], HALVES, P).transpose(0, 4, 3, 1, 2)

    kv_w = l0["kv_w"].reshape(C, C, 2)
    kv_b = l0["kv_b"].reshape(C, 2)
    weights = {"q": l0["q_w"], "k": kv_w[:, :, 0], "v": kv_w[:, :, 1], "o": l0["out_w"], "w1": l0["mlp_w1"],
               "maa1": l1["maa_w1"], "td1": l1["td_w1"], "Wr": l1["Wr"].T, "Wk": l1["Wk"].T, "Wv": l1["Wv"].T, "Wg": l1["Wg"].T,
               "Wo": l1["Wo"].T, "Wfk": l1["Wfk"].T, "Wfr": l1["Wfr"].T, "Wfv": l1["Wfv"].T}
    parity = (np.arange(P) // DH) % 2
    even, odd = (parity == 0).astype(np.float32), (parity == 1).astype(np.float32)
    vectors = {"q_b": l0["q_b"], "k_b": kv_b[:, 0], "v_b": kv_b[:, 1], "o_b": l0["out_b"], "pn": l0["postnorm_w"], "b1": l0["mlp_b1"],
               "b2": l0["mlp_b2"], "ln1_w": l1["ln1_w"], "ln1_b": l1["ln1_b"], "ln2_w": l1["ln2_w"], "ln2_b": l1["ln2_b"],
               "maa_x": l1["maa_x"], "maa": l1["maa_stack"].reshape(-1), "td": l1["time_decay"], "gn_w": l1["gn_w"], "gn_b": l1["gn_b"],
               "fk": l1["ffn_maa_k"], "fr": l1["ffn_maa_r"], "u": l1["u"].reshape(-1),
               "even": even, "odd": odd, "even16": even / np.float32(DH), "odd16": odd / np.float32(DH),
               "eps6": np.full(P, 1e-6, np.float32), "eps5": np.full(P, 1e-5, np.float32)}
    p = np.arange(P)
    same = (p[:, None] // RH == p[None, :] // RH).astype(np.float32)
    center = np.eye(P, dtype=np.float32) - same / np.float32(RH)
    mats = {"ident": np.eye(P, dtype=np.float32), "mean256": np.full((P, P), 1 / C, np.float32), "mean8": same / np.float32(RH),
            "center8": center, "same_head": same}
    for j in range(RH):
        mats[f"gather{j}"] = (same * ((p[None, :] % RH == j) - np.float32(1 / RH))).astype(np.float32)
    maa2 = np.zeros((P, MIX, C), np.float32)
    for f in range(MIX):
        row = DM * f % P
        maa2[row:row + DM, f, :] = l1["maa_w2"][f]
    td2 = np.zeros((P, C), np.float32)
    td2[0:DD] = l1["td_w2"]
    arrays = {
        "hT": grouped(np.concatenate([ctx, x], axis=1)),
        "xT": grouped(x).reshape(GROUPS, P, HALVES, T),
        "maskT": a["mask_BxS2_ik0"].reshape(GROUPS, T),
        "stT": grouped(ctx[:, 0:2]).transpose(0, 1, 4, 2, 3),
        "s0T": ctx[:, 2:2 + RH].reshape(GROUPS, GB, HALVES, P, RH).transpose(0, 3, 4, 2, 1),
        "W": np.concatenate([halves(weights[n]) for n in W_COLS], axis=2),
        "W2": l0["mlp_w2"].reshape(FM, P, C).transpose(1, 0, 2),
        "MAA2": maa2,
        "TD2": td2,
        "VEC": np.concatenate([vectors[n].reshape(-1, P).T for n in V_COLS], axis=1),
        "MATS": np.stack([mats[n] for n in M_NAMES], axis=1),
    }
    nc = bacc.Bacc("TRN2", target_bir_lowering=False, num_devices=1)
    arrays = {n: np.ascontiguousarray(z) for n, z in arrays.items()}
    args = {n: nc.dram_tensor(n, list(z.shape), my.dt.from_np(z.dtype), kind="ExternalInput").ap() for n, z in arrays.items()}
    out = nc.dram_tensor("out", [GROUPS, P, HALVES, T], my.dt.float32, kind="ExternalOutput").ap()
    build(nc, *[args[n] for n in ("hT", "xT", "maskT", "stT", "s0T", "W", "W2", "MAA2", "TD2", "VEC", "MATS")], out)
    r = run_bass_kernel_spmd(nc, [arrays], core_ids=[0])
    got = r.results[0]["out"]
    return got.reshape(GROUPS, P, HALVES, GB, S).transpose(0, 3, 4, 2, 1).reshape(B, S, C)
```

```python
import concourse.bass as bass
from concourse import mybir
from contextlib import ExitStack

B, S, C = 64, 64, 256
P = 128
HALVES = C // P
GB = 4
GROUPS = B // GB
T = GB * S
KEYS = 2 * S
HEADS, DH = 16, 16
PAIRS = P // (2 * DH)
UNITS = (GB // 2) * PAIRS
F = 4 * C
FM = F // P
RH = 8
QUARTERS = 4
DM, DD = 32, 64
MIX = 5
ORDER = (1, 0, 2, 3, 4)
FIRST = 0
NEG = -1e30

W_COLS = {}
at = 0
for _name, _n in (("q", C), ("k", C), ("v", C), ("o", C), ("w1", F), ("maa1", MIX * DM), ("td1", DD),
                  ("Wr", C), ("Wk", C), ("Wv", C), ("Wg", C), ("Wo", C), ("Wfk", C), ("Wfr", C), ("Wfv", C)):
    W_COLS[_name] = (at, at + _n)
    at += _n
W_TOTAL = at
W_PARTS = (("q", "v"), ("o", "w1"), ("maa1", "Wfv"))

V_COLS = {}
at = 0
for _name, _n in (("q_b", 2), ("k_b", 2), ("v_b", 2), ("o_b", 2), ("pn", 2), ("b1", FM), ("b2", 2), ("ln1_w", 2), ("ln1_b", 2),
                  ("ln2_w", 2), ("ln2_b", 2), ("maa_x", 2), ("maa", 2 * MIX), ("td", 2), ("gn_w", 2), ("gn_b", 2),
                  ("fk", 2), ("fr", 2), ("u", 2), ("even", 1), ("odd", 1), ("even16", 1), ("odd16", 1), ("eps6", 1), ("eps5", 1)):
    V_COLS[_name] = at
    at += _n
V_TOTAL = at

M_NAMES = ["ident", "mean256", "mean8"] + [f"expand{n}_{c}" for n in (RH, C) for c in range(QUARTERS)] + [ "center8", "same_head"] + [f"gather{j}" for j in range(RH)]
M_COL = {n: i for i, n in enumerate(M_NAMES)}


def slots(names, banks):
    return {n: (banks[i], banks[:i].count(banks[i])) for i, n in enumerate(names)}, [banks.count(b) for b in range(max(banks) + 1)]


A_NAMES = ([("q",), ("k", 0), ("k", 1), ("v", 0), ("v", 1)] + [("s", u) for u in range(UNITS)]
           + [("o",), ("rms",), ("rrms",)] + [("w1", n) for n in range(FM // 2)])
A_BANKS = [1, 0, 1, 0, 1] + [u % 2 for u in range(UNITS)] + [0, 1, 0] + [1, 0, 1, 0]
A_SLOT, A_USES = slots(A_NAMES, A_BANKS)
R_NAMES = [("mean", 0), ("var", 0), ("rstd", 0), ("maa",), ("x", 0), ("x", 1), ("td1",), ("x", 2), ("td2",), ("K",), ("x", 3), ("V",),
           ("x", 4), ("R",), ("G",), ("coef",), ("gvar",), ("grstd",), ("O",)]
TAIL_NAMES = [("mean", 1), ("var", 1), ("rstd", 1), ("fk",), ("fr",), ("fv",)]
R_SLOT, R_USES = slots(R_NAMES + TAIL_NAMES, [i % 2 for i in range(len(R_NAMES))] + [2] * len(TAIL_NAMES))

TURN = [("A", "va1"), ("A", "in2"), ("R", "mean0"), ("A", "in3"), ("R", "cent0"), ("A", "tr2"), ("A", "sc4"), ("A", "tr3"),
        ("R", "var0"), ("A", "sc5"), ("A", "va2"), ("A", "va3"), ("R", "rstd0"), ("A", "in4"), ("A", "tr4"), ("R", "norm0"),
        ("A", "in5"), ("R", "shift0"), ("A", "at0"), ("A", "sc6"), ("A", "sc7"), ("A", "tr5"), ("R", "maa"), ("A", "in6"),
        ("T", "mean1"), ("A", "in7"), ("T", "cent1"), ("A", "va4"), ("A", "tr6"), ("A", "va5"), ("R", "x0"), ("R", "x1"),
        ("T", "var1"), ("A", "tr7"), ("R", "td1"), ("A", "va6"), ("A", "va7"), ("T", "rstd1"), ("R", "x2"), ("T", "norm1"),
        ("R", "td2"), ("A", "at1"), ("R", "K"), ("T", "shift1"), ("A", "o"), ("R", "x3"), ("R", "decay"), ("R", "V"),
        ("R", "x4"), ("T", "fk"), ("R", "R"), ("T", "fr"), ("R", "rk"), ("A", "rms"), ("R", "s0"), ("R", "G"), ("T", "fv"),
        ("R", "g0"), ("R", "s1"), ("R", "s2"), ("R", "g1"), ("A", "rrms"), ("R", "s3"), ("A", "yn"), ("R", "g2"),
        ("A", "w0"), ("A", "w1"), ("R", "s4"), ("R", "g3"), ("A", "c0"), ("R", "g4"), ("R", "s5"), ("A", "c1"), ("R", "s6"),
        ("R", "s7"), ("R", "gate"), ("R", "coef"), ("A", "w2"), ("R", "g5"), ("A", "w3"), ("R", "g6"), ("R", "g7"),
        ("T", "fin"), ("N", "q"), ("R", "cen"), ("N", "k"), ("N", "v0"), ("R", "gn"), ("A", "c2"), ("N", "v1"),
        ("R", "grstd"), ("R", "gnorm"), ("N", "sc0"), ("N", "sc1"), ("R", "O"), ("R", "res"), ("A", "c3"), ("N", "in0"),
        ("A", "x1"), ("N", "in1"), ("N", "sc2"), ("N", "tr0"), ("N", "sc3"), ("N", "tr1"), ("N", "va0")]


def build(nc, hT, xT, maskT, stT, s0T, W, W2, MAA2, TD2, VEC, MATS, out):
    fp32, bf16, i32 = mybir.dt.float32, mybir.dt.bfloat16, mybir.dt.int32
    ALU, ACT, AX = mybir.AluOpType, mybir.ActivationFunctionType, mybir.AxisListType

    with ExitStack() as ctx:
        def sb(name, shape, dt=fp32):
            return ctx.enter_context(nc.sbuf_tensor(name, shape, dt))

        class Event:
            def __init__(self, name, per_group):
                self.sem, self.n = ctx.enter_context(nc.semaphore(name)), per_group

        def count(event, g, k):
            value = g * event.n + k
            return max(value, 0) if isinstance(value, int) else value

        w_sb = sb("w_sb", [P, HALVES, W_TOTAL])
        w2_sb = sb("w2_sb", [P, FM, C])
        maa2_sb = sb("maa2_sb", [P, MIX, C])
        td2_sb = sb("td2_sb", [P, C])
        vec = sb("vec", [P, V_TOTAL])
        mats = sb("mats", [P, len(M_NAMES), P])
        bonus_w = sb("bonus_w", [P, HALVES, P])
        q_bias = sb("q_bias", [P, 2, HALVES])
        o_bias = sb("o_bias", [P, HALVES])
        ones_bf = sb("ones_bf", [P, P], bf16)

        def w(name, k, a=0, b=None):
            lo, hi = W_COLS[name]
            return w_sb[:, k, lo + a:(hi if b is None else lo + b)]

        def v(name, i=0):
            c = V_COLS[name] + i
            return vec[:, c:c + 1]

        def mat(name):
            return mats[:, M_COL[name], :]

        h_sb = sb("h_sb", [P, HALVES, GB, KEYS])
        xa_sb = sb("xa_sb", [P, HALVES, T])
        mask_i = sb("mask_i", [P, GB, S], i32)
        mask_b = sb("mask_b", [P, GB, S], bf16)
        qt = sb("qt", [P, HALVES, GB, 2, S])
        kt = sb("kt", [P, HALVES, GB, KEYS])
        vv = sb("vv", [P, GB, C])
        neg_max = sb("neg_max", [P, 2, 4])
        sums = sb("sums", [P, 2, 4])
        rsum = sb("rsum", [P, 2, 4])
        probs = sb("probs", [P, 3, 4, KEYS])
        probs_t = sb("probs_t", [P, 2, 4, P])
        o_even = sb("o_even", [P, 4, S])
        attn = sb("attn", [P, GB, HALVES, S])
        y = sb("y", [P, HALVES, T])
        ysq = sb("ysq", [P, HALVES, T])
        ysum = sb("ysum", [P, T])
        a_ms = sb("a_ms", [P, T // QUARTERS])
        hid = sb("hid", [P, 2, 2, T])
        x1 = sb("x1", [P, HALVES, T])

        st_sb = [sb(f"st_sb{n}", [P, HALVES, GB]) for n in range(2)]
        s0_sb = sb("s0_sb", [P, RH, HALVES, GB])
        xc = [sb(f"xc{n}", [P, HALVES, T]) for n in range(2)]
        sq = [sb(f"sq{n}", [P, HALVES, T]) for n in range(2)]
        hsum = [sb(f"hsum{n}", [P, T]) for n in range(2)]
        r_ms = [sb(f"r_ms{n}", [P, T // QUARTERS]) for n in range(2)]
        xs = [sb(f"xs{n}", [P, HALVES, GB, S + 1]) for n in range(2)]
        sx = [sb(f"sx{n}", [P, HALVES, T]) for n in range(2)]
        z = sb("z", [P, HALVES, T])
        th = sb("th", [P, 2, T])
        tmp = sb("tmp", [P, 2, HALVES, T])
        xm = sb("xm", [P, 2, HALVES, T])
        tw = sb("tw", [P, T])
        e1 = sb("e1", [P, HALVES, T])
        decay = sb("decay", [P, HALVES, GB, S])
        rr = sb("rr", [P, HALVES, T])
        kk = sb("kk", [P, HALVES, T])
        vr = sb("vr", [P, HALVES, T])
        gt = sb("gt", [P, HALVES, T])
        gate = sb("gate", [P, HALVES, T])
        kv = sb("kv", [P, RH, HALVES * GB, S])
        vb = sb("vb", [P, RH, HALVES * T])
        st = sb("st", [P, 2, HALVES * T])
        rs = sb("rs", [P, 4, HALVES * T])
        rk, bonus, og, gsq, g_ms = tmp[:, 1, :, :], z, xc[0], sq[0], e1[:, 0, 0:HALVES * T // QUARTERS]
        x2 = sb("x2", [P, HALVES, T])
        xf = sb("xf", [P, 2, HALVES, T])
        tr = sb("tr", [P, HALVES, T])
        relu, act, ft = xc[1], sq[1], sx[1]

        psum = [ctx.enter_context(nc.psum_tensor(f"bank{i}", [P, 512], fp32)) for i in range(8)]
        A_BANK, R_BANK = psum[0:2], psum[4:7]
        pt_ps, o_ps, red_ps = psum[2], psum[3], psum[7]

        def flat(t):
            return t[:, :, :].rearrange("p h t -> p (h t)")

        def by_batch(ap):
            return ap.rearrange("p (b s) -> p b s", b=GB)

        def batches(ap):
            return ap.rearrange("p (b s) -> p b s", s=S)

        def both(ap):
            return ap.unsqueeze(1).broadcast_to([P, HALVES, T])

        def vr_rows(j):
            return flat(vr)[j:P:RH, :].unsqueeze(1).broadcast_to([P // RH, RH, HALVES * T])

        ld_vec, ld_mats, ld_w2, ld_small = (Event(n, 0) for n in ("vec_in", "mats_in", "w2_in", "small_in"))
        ld_w = [Event(f"weights_in{i}", 0) for i in range(3)]
        fills, folded, bias_sum = Event("fills", 0), Event("folded", 0), Event("bias_sum", 0)
        h_in, xa_in, mask_in, s0_in = (Event(n, 16) for n in ("h_in", "xa_in", "mask_in", "s0_in"))
        st_in = [Event(f"st_in{n}", 16) for n in range(2)]
        out_done = Event("out_done", 16)
        a_full = [Event(f"a_full{i}", A_USES[i]) for i in range(2)]
        a_free = [Event(f"a_free{i}", A_USES[i]) for i in range(2)]
        r_full = [Event(f"r_full{i}", R_USES[i]) for i in range(3)]
        r_free = [Event(f"r_free{i}", R_USES[i]) for i in range(3)]
        pt_full, pt_free = Event("pt_full", UNITS), Event("pt_free", UNITS)
        o_full, o_free = Event("o_full", BPS + 1), Event("o_free", BPS + 1)
        red_full = Event("red_full", 1)
        mask_made = Event("mask_made", 1)
        max_made, rsum_made, norm_made = (Event(n, UNITS) for n in ("max_made", "rsum_made", "norm_made"))
        o_even_made = Event("o_even_made", BPS)
        ysq_made, ysum_made, arstd_made = (Event(n, 1) for n in ("ysq_made", "ysum_made", "arstd_made"))
        sq_made, rstd_made, xs_made, row_made, sx_made = ([Event(f"{name}{n}", 1) for n in range(2)] for name in (
            "sq_made", "rstd_made", "xs_made", "row_made", "sx_made"))
        hsum_made = [Event(f"hsum_made{n}", 2) for n in range(2)]
        z_made, xm_made = Event("z_made", 1), Event("xm_made", MIX)
        decay_made, gt_made = Event("decay_made", 1), Event("gt_made", 1)
        first_made, kv_made, st_made, rs_made = Event("first_made", 1), Event("kv_made", RH), Event("st_made", RH), Event("rs_made", RH)
        gathered = Event("gathered", RH)
        vb_in = [Event(f"vb_in{j}", 16) for j in range(RH)]
        rk_made = Event("rk_made", 1)
        gate_made, gate_b_made, gsq_made, gated = (Event(n, 1) for n in ("gate_made", "gate_b_made", "gsq_made", "gated"))
        grstd_made, og_made = (Event(n, 1) for n in ("grstd_made", "og_made"))
        shift_made, act_made, fin_made = Event("shift_made", 2), Event("act_made", 1), Event("fin_made", 1)

        def a_bank(*name):
            return A_BANK[A_SLOT[name][0]]

        def a_open(g, *name):
            b, use = A_SLOT[name]
            return a_free[b].sem, count(a_free[b], g, use)

        def a_ready(g, *name):
            b, use = A_SLOT[name]
            return a_full[b].sem, count(a_full[b], g, use + 1)

        def a_taken(g, *name):
            b, use = A_SLOT[name]
            return a_free[b].sem, count(a_free[b], g, use + 1)

        def a_filled(*name):
            return a_full[A_SLOT[name][0]].sem

        def a_read(*name):
            return a_free[A_SLOT[name][0]].sem

        def r_bank(*name):
            return R_BANK[R_SLOT[name][0]]

        def r_open(g, *name):
            b, use = R_SLOT[name]
            return r_free[b].sem, count(r_free[b], g, use)

        def r_ready(g, *name):
            b, use = R_SLOT[name]
            return r_full[b].sem, count(r_full[b], g, use + 1)

        def r_taken(g, *name):
            b, use = R_SLOT[name]
            return r_free[b].sem, count(r_free[b], g, use + 1)

        def r_filled(*name):
            return r_full[R_SLOT[name][0]].sem

        def r_read(*name):
            return r_free[R_SLOT[name][0]].sem

        def run(eng, attention, recurrent):
            def turn(i, streams="NART"):
                for stream, piece in TURN:
                    if stream not in streams:
                        continue
                    if stream == "N":
                        attention(i + 1, piece)
                    elif stream == "A":
                        attention(i, piece)
                    elif stream == "R":
                        recurrent(i - 1, piece)
                    else:
                        recurrent(i - 2, piece)

            for stream, piece in TURN:
                if stream == "N":
                    attention(FIRST, piece)
            turn(0, "NA")
            turn(1, "NAR")
            turn(2)
            with eng.Fori(3, GROUPS - 1) as i:
                turn(i)
            turn(GROUPS - 1, "ART")
            turn(GROUPS, "RT")
            turn(GROUPS + 1, "T")

        block = ctx.enter_context(nc.Block())

        @block.sync
        def _(sp):
            def load_attention(g):
                b, use = A_SLOT[("v", 1)]
                sp.wait_ge(a_full[b].sem, count(a_full[b], g - 1, use + 1))
                sp.dma_start(h_sb[:, :, :, :], hT[g, :, :, :, :]).then_inc(h_in.sem, 16)
                sp.wait_ge(mask_made.sem, count(mask_made, g, 0))
                sp.dma_start(mask_i[:, :, :].rearrange("p b s -> p (b s)"), maskT[g, :].partition_broadcast(P)).then_inc(mask_in.sem, 16)

            def load_residual(g):
                sp.wait_ge(o_free.sem, count(o_free, g, 0))
                sp.dma_start(xa_sb[:, :, :], xT[g, :, :, :]).then_inc(xa_in.sem, 16)

            def load_row(g, n):
                sp.wait_ge(row_made[n].sem, count(row_made[n], g, 0))
                sp.dma_start(st_sb[n][:, :, :], stT[g, :, 1 - n, :, :]).then_inc(st_in[n].sem, 16)

            def load_state(g):
                load_row(g, 0)
                sp.wait_ge(first_made.sem, count(first_made, g, 0))
                sp.dma_start(s0_sb[:, :, :, :], s0T[g, :, :, :, :]).then_inc(s0_in.sem, 16)

            def spread(g):
                sp.wait_ge(*r_taken(g, "V"))
                for j in range(RH):
                    sp.dma_start(vb[:, j, :], vr_rows(j)).then_inc(vb_in[j].sem, 16)

            def store(g):
                sp.wait_ge(fin_made.sem, count(fin_made, g, 1))
                sp.dma_start(out[g, :, :, :], x2[:, :, :]).then_inc(out_done.sem, 16)

            def load_weights(n):
                lo, hi = W_COLS[W_PARTS[n][0]][0], W_COLS[W_PARTS[n][1]][1]
                sp.dma_start(w_sb[:, :, lo:hi], W[:, :, lo:hi]).then_inc(ld_w[n].sem, 16)

            sp.dma_start(vec[:, :], VEC[:, :]).then_inc(ld_vec.sem, 16)
            load_weights(0)
            load_attention(0)
            sp.dma_start(mats[:, :, :], MATS[:, :, :]).then_inc(ld_mats.sem, 16)
            load_weights(1)
            load_residual(0)
            sp.dma_start(w2_sb[:, :, :], W2[:, :, :]).then_inc(ld_w2.sem, 16)
            load_weights(2)
            sp.dma_start(maa2_sb[:, :, :], MAA2[:, :, :]).then_inc(ld_small.sem, 16)
            sp.dma_start(td2_sb[:, :], TD2[:, :]).then_inc(ld_small.sem, 16)
            load_attention(1)
            load_state(0)
            load_residual(1)

            def turn(i, last=False):
                if not last:
                    load_attention(i + 1)
                load_row(i - 1, 1)
                spread(i - 1)
                store(i - 2)
                load_state(i)
                if not last:
                    load_residual(i + 1)

            load_row(0, 1)
            spread(0)
            load_attention(2)
            load_state(1)
            load_residual(2)
            turn(2)
            with sp.Fori(3, GROUPS - 1) as i:
                turn(i)
            turn(GROUPS - 1, last=True)
            load_row(GROUPS - 1, 1)
            spread(GROUPS - 1)
            store(GROUPS - 2)
            store(GROUPS - 1)
            sp.wait_ge(out_done.sem, 16 * GROUPS)

        @block.tensor
        def _(pe):
            mm = nc.tensor.matmul

            def project(bank, name, rhs, blocks=(0, 1), widths=(P, P)):
                for n, (m, width) in enumerate(zip(blocks, widths)):
                    for k in range(HALVES):
                        last = mm(bank[0:width, n * T:(n + 1) * T], w(name, k, m * P, m * P + width), rhs[k], start=(k == 0), stop=(k == 1))
                return last

            def average(bank, src):
                return mm(bank[:, 0:T], mat("mean256"), src[:, :], start=True, stop=True)

            def average_by_quarter(bank, src):
                n = T // QUARTERS
                for c in range(QUARTERS):
                    last = mm(bank[32 * c:32 * c + 32, 0:n], mat("mean256")[:, 0:32], src[:, c * n:(c + 1) * n], start=True, stop=True)
                return last

            def expand(bank, name, src, n):
                for c in range(QUARTERS):
                    last = mm(bank[:, c * n:(c + 1) * n], mat(f"{name}_{c}"), src[:, :], start=True, stop=True)
                return last

            def scores(g, u):
                bp, r = unit(u)
                bank = a_bank("s", u)
                pe.wait_ge(*a_open(g, "s", u))
                rows = slice(32 * r, 32 * r + 32)
                for n in range(4):
                    b, h = 2 * bp + n // 2, n % 2
                    mm(bank[:, n * P:(n + 1) * P], qt[rows, h, b, :, :].rearrange("p e s -> p (e s)"), kt[rows, h, b, :],
                       start=(n == 0), stop=False, skip_group_check=True)
                row = slice(32 * r, 32 * r + 1)
                for n in range(4):
                    last = mm(bank[:, n * P:n * P + S], ones_bf[row, :], mask_b[row, 2 * bp + n // 2, :],
                              start=False, stop=True, skip_group_check=True)
                last.then_inc(a_filled("s", u), 1)

            def transpose(g, u):
                pe.wait_ge(norm_made.sem, count(norm_made, g, u + 1))
                pe.wait_ge(pt_free.sem, count(pt_free, g, u))
                for n in range(4):
                    last = nc.tensor.transpose(pt_ps[:, n * P:(n + 1) * P], probs[:, PROBS(u), n, :], mat("ident"))
                last.then_inc(pt_full.sem, 1)

            def values(g, u):
                bp, r = unit(u)
                pe.wait_ge(pt_free.sem, count(pt_free, g, u + 1))
                if r == 0:
                    pe.wait_ge(o_free.sem, count(o_free, g, bp))
                for n in range(4):
                    b, h = 2 * bp + n // 2, n % 2
                    last = mm(o_ps[32 * r:32 * r + 32, n * P:(n + 1) * P], vv[:, b, h * P + 32 * r:h * P + 32 * r + 32],
                              probs_t[:, u % 2, n, :], start=True, stop=True)
                if r == PAIRS - 1:
                    last.then_inc(o_full.sem, 1)

            def attention(g, piece):
                if piece == "q":
                    if g is FIRST:
                        pe.wait_ge(ld_w[0].sem, 16)
                    pe.wait_ge(h_in.sem, count(h_in, g, 16))
                    pe.wait_ge(*a_open(g, "q"))
                    project(a_bank("q"), "q", [h_sb[:, k, :, S:KEYS] for k in range(HALVES)]).then_inc(a_filled("q"), 1)
                elif piece == "k":
                    for m in range(2):
                        pe.wait_ge(*a_open(g, "k", m))
                        for k in range(HALVES):
                            last = mm(a_bank("k", m)[:, :], w("k", k, m * P, m * P + P), h_sb[:, k, :, :], start=(k == 0), stop=(k == 1))
                        last.then_inc(a_filled("k", m), 1)
                elif piece in ("v0", "v1"):
                    n = int(piece[1])
                    bank = a_bank("v", n)
                    pe.wait_ge(*a_open(g, "v", n))
                    for i in range(2):
                        for k in range(HALVES):
                            last = mm(bank[:, i * C:(i + 1) * C], h_sb[:, k, 2 * n + i, :], w("v", k), start=(k == 0), stop=(k == 1))
                    last.then_inc(a_filled("v", n), 1)
                    if g is FIRST and n == 1:
                        pe.wait_ge(ld_mats.sem, 16)
                        pe.wait_ge(fills.sem, FILLS)
                        pe.wait_ge(ld_w[1].sem, 16)
                        for m in range(2):
                            for k in range(2):
                                last = mm(red_ps[:, m:m + 1], w("o", k, m * P, m * P + P), v("v_b", k), start=(k == 0), stop=(k == 1))
                        last.then_inc(bias_sum.sem, 1)
                elif piece[0:2] == "sc":
                    u = int(piece[2:])
                    if u == 0:
                        pe.wait_ge(mask_made.sem, count(mask_made, g, 1))
                        pe.wait_ge(*a_taken(g, "k", 1))
                    scores(g, u)
                elif piece[0:2] == "tr":
                    transpose(g, int(piece[2:]))
                elif piece[0:2] == "va":
                    u = int(piece[2:])
                    if u == 0:
                        for n in range(2):
                            pe.wait_ge(*a_taken(g, "v", n))
                    values(g, u)
                elif piece == "o":
                    pe.wait_ge(o_free.sem, count(o_free, g, BPS))
                    pe.wait_ge(*a_open(g, "o"))
                    project(a_bank("o"), "o", [attn[:, :, k, :] for k in range(HALVES)]).then_inc(a_filled("o"), 1)
                elif piece == "rms":
                    pe.wait_ge(ysum_made.sem, count(ysum_made, g, 1))
                    pe.wait_ge(*a_open(g, "rms"))
                    average_by_quarter(a_bank("rms"), ysum).then_inc(a_filled("rms"), 1)
                elif piece == "rrms":
                    pe.wait_ge(arstd_made.sem, count(arstd_made, g, 1))
                    pe.wait_ge(*a_open(g, "rrms"))
                    expand(a_bank("rrms"), "expand256", a_ms, T // QUARTERS).then_inc(a_filled("rrms"), 1)
                elif piece[0] == "w":
                    n = int(piece[1])
                    if n == 0:
                        if g is FIRST:
                            pe.wait_ge(folded.sem, FOLDS)
                            pe.wait_ge(ld_w2.sem, 16)
                        pe.wait_ge(*a_taken(g, "rrms"))
                    pe.wait_ge(*a_open(g, "w1", n))
                    project(a_bank("w1", n), "w1", [y[:, k, :] for k in range(HALVES)], (2 * n, 2 * n + 1)).then_inc(a_filled("w1", n), 1)
                elif piece[0] == "c":
                    n = int(piece[1])
                    pe.wait_ge(*a_taken(g, "w1", n))
                    for i in range(2):
                        for m in range(HALVES):
                            last = mm(o_ps[:, m * T:(m + 1) * T], w2_sb[:, 2 * n + i, m * P:(m + 1) * P], hid[:, n % 2, i, :],
                                      start=(n == 0 and i == 0 and m == 0), stop=(n == FM // 2 - 1 and i == 1), skip_group_check=True)
                    if n == FM // 2 - 1:
                        last.then_inc(o_full.sem, 1)

            def shifted(n):
                return [xm[:, n % 2, k, :] for k in range(HALVES)]

            def gather(g, j):
                if j == 0:
                    pe.wait_ge(gated.sem, count(gated, g, 0))
                pe.wait_ge(rs_made.sem, count(rs_made, g, j + 1))
                mm(red_ps[:, :], mat(f"gather{j}"), rs[:, j % 4, :], start=(j == 0), stop=False).then_inc(gathered.sem, 1)

            def recurrent(g, piece):
                if piece in ("mean0", "mean1"):
                    n = int(piece[-1])
                    pe.wait_ge(hsum_made[n].sem, count(hsum_made[n], g, 1))
                    pe.wait_ge(*r_open(g, "mean", n))
                    average(r_bank("mean", n), hsum[n]).then_inc(r_filled("mean", n), 1)
                elif piece in ("var0", "var1"):
                    n = int(piece[-1])
                    pe.wait_ge(hsum_made[n].sem, count(hsum_made[n], g, 2))
                    pe.wait_ge(*r_open(g, "var", n))
                    average_by_quarter(r_bank("var", n), hsum[n]).then_inc(r_filled("var", n), 1)
                elif piece in ("rstd0", "rstd1"):
                    n = int(piece[-1])
                    pe.wait_ge(rstd_made[n].sem, count(rstd_made[n], g, 1))
                    pe.wait_ge(*r_open(g, "rstd", n))
                    expand(r_bank("rstd", n), "expand256", r_ms[n], T // QUARTERS).then_inc(r_filled("rstd", n), 1)
                elif piece == "maa":
                    pe.wait_ge(ld_w[2].sem, 16)
                    pe.wait_ge(ld_small.sem, 32)
                    pe.wait_ge(z_made.sem, count(z_made, g, 1))
                    pe.wait_ge(*r_open(g, "maa"))
                    project(r_bank("maa"), "maa1", [z[:, k, :] for k in range(HALVES)], (0, 1), (P, DM)).then_inc(r_filled("maa"), 1)
                elif piece[0] == "x":
                    n = int(piece[1])
                    if n == 0:
                        pe.wait_ge(*r_taken(g, "maa"))
                    bank = r_bank("x", n)
                    pe.wait_ge(*r_open(g, "x", n))
                    for m in range(HALVES):
                        last = mm(bank[:, m * T:(m + 1) * T], maa2_sb[:, ORDER[n], m * P:(m + 1) * P], th[:, ORDER[n] // 4, :], start=True, stop=True)
                    last.then_inc(r_filled("x", n), 1)
                elif piece == "td1":
                    pe.wait_ge(xm_made.sem, count(xm_made, g, 1))
                    pe.wait_ge(*r_open(g, "td1"))
                    project(r_bank("td1"), "td1", shifted(0), (0,), (DD,)).then_inc(r_filled("td1"), 1)
                elif piece == "td2":
                    pe.wait_ge(*r_taken(g, "td1"))
                    pe.wait_ge(*r_open(g, "td2"))
                    for m in range(HALVES):
                        last = mm(r_bank("td2")[:, m * T:(m + 1) * T], td2_sb[:, m * P:(m + 1) * P], tw[:, :], start=True, stop=True)
                    last.then_inc(r_filled("td2"), 1)
                elif piece in "KVRG":
                    n = "KVRG".index(piece) + 1
                    pe.wait_ge(xm_made.sem, count(xm_made, g, n + 1))
                    pe.wait_ge(*r_open(g, piece))
                    project(r_bank(piece), "W" + piece.lower(), shifted(n)).then_inc(r_filled(piece), 1)
                elif piece[0] == "g" and piece[1].isdigit():
                    gather(g, int(piece[1]))
                elif piece == "coef":
                    pe.wait_ge(rk_made.sem, count(rk_made, g, 1))
                    pe.wait_ge(*r_open(g, "coef"))
                    for m in range(HALVES):
                        last = mm(r_bank("coef")[:, m * T:(m + 1) * T], bonus_w[:, m, :], rk[:, m, :], start=True, stop=True)
                    last.then_inc(r_filled("coef"), 1)
                elif piece == "cen":
                    pe.wait_ge(*r_taken(g, "coef"))
                    mm(red_ps[:, :], mat("center8"), flat(bonus), start=False, stop=True).then_inc(red_full.sem, 1)
                elif piece == "gn":
                    pe.wait_ge(gsq_made.sem, count(gsq_made, g, 1))
                    pe.wait_ge(*r_open(g, "gvar"))
                    n = HALVES * T // QUARTERS
                    for c in range(QUARTERS):
                        last = mm(r_bank("gvar")[32 * c:32 * c + 32, 0:n], mat("mean8")[:, 0:32], flat(gsq)[:, c * n:(c + 1) * n], start=True, stop=True)
                    last.then_inc(r_filled("gvar"), 1)
                elif piece == "grstd":
                    pe.wait_ge(grstd_made.sem, count(grstd_made, g, 1))
                    pe.wait_ge(*r_open(g, "grstd"))
                    expand(r_bank("grstd"), "expand8", g_ms, HALVES * T // QUARTERS).then_inc(r_filled("grstd"), 1)
                elif piece == "O":
                    pe.wait_ge(og_made.sem, count(og_made, g, 1))
                    pe.wait_ge(*r_open(g, "O"))
                    project(r_bank("O"), "Wo", [og[:, k, :] for k in range(HALVES)]).then_inc(r_filled("O"), 1)
                elif piece in ("fk", "fr"):
                    n = ("fk", "fr").index(piece)
                    pe.wait_ge(shift_made.sem, count(shift_made, g, n + 1))
                    pe.wait_ge(*r_open(g, piece))
                    project(r_bank(piece), "W" + piece, [xf[:, n, k, :] for k in range(HALVES)]).then_inc(r_filled(piece), 1)
                elif piece == "fv":
                    pe.wait_ge(act_made.sem, count(act_made, g, 1))
                    pe.wait_ge(*r_open(g, "fv"))
                    project(r_bank("fv"), "Wfv", [act[:, k, :] for k in range(HALVES)]).then_inc(r_filled("fv"), 1)

            run(pe, attention, recurrent)

        @block.scalar
        def _(sc):
            fn = nc.scalar.activation

            def attention(g, piece):
                if piece == "k":
                    if g is FIRST:
                        sc.wait_ge(ld_vec.sem, 16)
                    for m in range(2):
                        sc.wait_ge(*a_ready(g, "k", m))
                        fn(kt[:, m, :, :].rearrange("p b s -> p (b s)"), a_bank("k", m)[:, :], ACT.Identity, bias=v("k_b", m)).then_inc(a_read("k", m), 1)
                elif piece in ("v0", "v1"):
                    n = int(piece[1])
                    sc.wait_ge(*a_ready(g, "v", n))
                    fn(vv[:, 2 * n:2 * n + 2, :].rearrange("p b s -> p (b s)"), a_bank("v", n)[:, :], ACT.Copy).then_inc(a_read("v", n), 1)
                elif piece[0:2] == "sc":
                    u = int(piece[2:])
                    sc.wait_ge(max_made.sem, count(max_made, g, u + 1))
                    sc.wait_ge(norm_made.sem, count(norm_made, g, max(u - 1, 0)))
                    sc.wait_ge(pt_full.sem, count(pt_full, g, max(u - 2, 0)))
                    bank = a_bank("s", u)
                    for n in range(4):
                        last = fn(probs[:, PROBS(u), n, :], bank[:, n * P:(n + 1) * P], ACT.Exp,
                                  bias=neg_max[:, u % 2, n:n + 1], accum_out=sums[:, u % 2, n:n + 1])
                    last.then_inc(a_read("s", u), 1)
                elif piece[0:2] == "at":
                    bp = int(piece[2:])
                    sc.wait_ge(o_full.sem, count(o_full, g, bp + 1))
                    sc.wait_ge(o_free.sem, count(o_free, g, bp))
                    fn(o_even[:, :, :], o_ps[:, :].rearrange("p (n e s) -> p n e s", n=4, e=2)[:, :, 0, :], ACT.Copy,
                       scale=v("even")).then_inc(o_even_made.sem, 1)
                elif piece == "o":
                    sc.wait_ge(*a_taken(g, "o"))
                    fn(ysq[:, :, :], y[:, :, :], ACT.Square).then_inc(ysq_made.sem, 1)
                elif piece == "rms":
                    sc.wait_ge(*a_ready(g, "rms"))
                    fn(a_ms[:, :], a_bank("rms")[:, 0:T // QUARTERS], ACT.Sqrt, bias=v("eps6")).then_inc(a_read("rms"), 1)
                elif piece[0] == "w":
                    n = int(piece[1])
                    sc.wait_ge(*a_ready(g, "w1", n))
                    for i in range(2):
                        last = fn(hid[:, n % 2, i, :], a_bank("w1", n)[:, i * T:(i + 1) * T], ACT.Gelu_apprx_tanh, bias=v("b1", 2 * n + i))
                    last.then_inc(a_read("w1", n), 1)

            def recurrent(g, piece):
                if piece in ("cent0", "cent1"):
                    n = int(piece[-1])
                    sc.wait_ge(*r_taken(g, "mean", n))
                    fn(sq[n][:, :, :], xc[n][:, :, :], ACT.Square).then_inc(sq_made[n].sem, 1)
                    sc.wait_ge(st_in[n].sem, count(st_in[n], g, 16))
                    sc.wait_ge(sx_made[n].sem, count(sx_made[n], g, 0))
                    fn(xs[n][:, :, :, 0], st_sb[n][:, :, :], ACT.Copy).then_inc(row_made[n].sem, 1)
                elif piece in ("var0", "var1"):
                    n = int(piece[-1])
                    sc.wait_ge(*r_ready(g, "var", n))
                    fn(r_ms[n][:, :], r_bank("var", n)[:, 0:T // QUARTERS], ACT.Sqrt, bias=v("eps5")).then_inc(r_read("var", n), 1)
                elif piece == "maa":
                    sc.wait_ge(*r_ready(g, "maa"))
                    fn(th[:, 0, :], r_bank("maa")[:, 0:T], ACT.Tanh)
                    fn(th[0:DM, 1, :], r_bank("maa")[0:DM, T:2 * T], ACT.Tanh).then_inc(r_read("maa"), 1)
                elif piece == "td1":
                    sc.wait_ge(*r_ready(g, "td1"))
                    fn(tw[0:DD, :], r_bank("td1")[0:DD, 0:T], ACT.Tanh).then_inc(r_read("td1"), 1)
                elif piece == "td2":
                    sc.wait_ge(*r_ready(g, "td2"))
                    for m in range(HALVES):
                        last = fn(e1[:, m, :], r_bank("td2")[:, m * T:(m + 1) * T], ACT.Exp, bias=v("td", m))
                    last.then_inc(r_read("td2"), 1)
                elif piece == "K":
                    copy(g, "K", kk)
                elif piece == "decay":
                    sc.wait_ge(*r_taken(g, "td2"))
                    fn(decay[:, :, :, :].rearrange("p h b s -> p (h b) s")[:, :, 1:S], batches(flat(e1))[:, :, 0:S - 1],
                       ACT.Exp, scale=-1.0).then_inc(decay_made.sem, 1)
                elif piece == "V":
                    sc.wait_ge(s0_in.sem, count(s0_in, g, 16))
                    sc.wait_ge(st_made.sem, count(st_made, g, 0))
                    fn(kv[:, :, :, 0], s0_sb[:, :, :, :].rearrange("p j h b -> p j (h b)"), ACT.Copy).then_inc(first_made.sem, 1)
                    copy(g, "V", vr)
                elif piece == "R":
                    copy(g, "R", rr)
                elif piece == "G":
                    sc.wait_ge(*r_ready(g, "G"))
                    fn(flat(gt), r_bank("G")[:, :], ACT.Tanh, scale=0.5).then_inc(gt_made.sem, 1)
                elif piece == "cen":
                    sc.wait_ge(red_full.sem, count(red_full, g, 1))
                    fn(flat(gsq), red_ps[:, :], ACT.Square).then_inc(gsq_made.sem, 1)
                elif piece == "gn":
                    sc.wait_ge(*r_ready(g, "gvar"))
                    fn(g_ms, r_bank("gvar")[:, 0:HALVES * T // QUARTERS], ACT.Sqrt, bias=v("eps5")).then_inc(r_read("gvar"), 1)
                elif piece == "fk":
                    sc.wait_ge(*r_ready(g, "fk"))
                    fn(flat(relu), r_bank("fk")[:, :], ACT.Relu).then_inc(r_read("fk"), 1)
                elif piece == "fr":
                    sc.wait_ge(*r_ready(g, "fr"))
                    fn(flat(tr), r_bank("fr")[:, :], ACT.Tanh, scale=0.5).then_inc(r_read("fr"), 1)

            def copy(g, name, to):
                sc.wait_ge(*r_ready(g, name))
                fn(flat(to), r_bank(name)[:, :], ACT.Copy).then_inc(r_read(name), 1)

            run(sc, attention, recurrent)

        @block.vector
        def _(ve):
            tt, ts, stt, invert = nc.vector.tensor_tensor, nc.vector.tensor_scalar, nc.vector.scalar_tensor_tensor, nc.vector.reciprocal

            def shift(to, n, name, event):
                for h in range(HALVES):
                    last = stt(by_batch(to[:, h, :]), by_batch(sx[n][:, h, :]), v(name, h), xs[n][:, h, :, 1:S + 1], ALU.mult, ALU.add)
                last.then_inc(event.sem, 1)

            def attention(g, piece):
                if piece == "q":
                    if g is FIRST:
                        ve.wait_ge(ld_vec.sem, 16)
                        for e, name in enumerate(("even16", "odd16")):
                            ts(q_bias[:, e, :], vec[:, V_COLS["q_b"]:V_COLS["q_b"] + 2], v(name), None, ALU.mult).then_inc(folded.sem, 1)
                        ve.wait_ge(folded.sem, 2)
                    ve.wait_ge(mask_in.sem, count(mask_in, g, 16))
                    ts(mask_b[:, :, :], mask_i[:, :, :], 0, NEG, ALU.is_equal, ALU.mult).then_inc(mask_made.sem, 1)
                    ve.wait_ge(*a_ready(g, "q"))
                    for m in range(HALVES):
                        for e, name in enumerate(("even16", "odd16")):
                            last = ts(qt[:, m, :, e, :], by_batch(a_bank("q")[:, m * T:(m + 1) * T]), v(name), q_bias[:, e, m:m + 1], ALU.mult, ALU.add)
                    last.then_inc(a_read("q"), 1)
                elif piece == "v1":
                    if g is FIRST:
                        ve.wait_ge(ld_w[1].sem, 16)
                        for k in range(2):
                            ts(w("w1", k), w("w1", k), v("pn", k), None, ALU.mult).then_inc(folded.sem, 1)
                        ve.wait_ge(bias_sum.sem, 1)
                        tt(o_bias[:, :], red_ps[:, 0:2], vec[:, V_COLS["o_b"]:V_COLS["o_b"] + 2], ALU.add).then_inc(folded.sem, 1)
                        ve.wait_ge(ld_mats.sem, 16)
                        for k in range(2):
                            ts(bonus_w[:, k, :], mat("same_head"), v("u", k), None, ALU.mult).then_inc(folded.sem, 1)
                elif piece[0:2] == "sc":
                    u = int(piece[2:])
                    ve.wait_ge(*a_ready(g, "s", u))
                    nc.vector.tensor_reduce(neg_max[:, u % 2, :], a_bank("s", u)[:, :].rearrange("p (n k) -> p n k", n=4), AX.X, ALU.max,
                                            negate=True).then_inc(max_made.sem, 1)
                elif piece[0:2] == "in":
                    u = int(piece[2:])
                    ve.wait_ge(*a_taken(g, "s", u))
                    invert(rsum[:, u % 2, :], sums[:, u % 2, :]).then_inc(rsum_made.sem, 1)
                elif piece[0:2] == "tr":
                    u = int(piece[2:])
                    ve.wait_ge(pt_full.sem, count(pt_full, g, u + 1))
                    nc.vector.tensor_copy(probs_t[:, u % 2, :, :].rearrange("p n q -> p (n q)"), pt_ps[:, :]).then_inc(pt_free.sem, 1)
                elif piece[0:2] == "at":
                    bp = int(piece[2:])
                    ve.wait_ge(o_even_made.sem, count(o_even_made, g, bp + 1))
                    stt(attn[:, 2 * bp:2 * bp + 2, :, :].rearrange("p b h s -> p (b h) s"),
                        o_ps[:, :].rearrange("p (n e s) -> p n e s", n=4, e=2)[:, :, 1, :], v("odd"), o_even[:, :, :],
                        ALU.mult, ALU.add).then_inc(o_free.sem, 1)
                    if g is FIRST and bp == BPS - 1:
                        ve.wait_ge(ld_w[2].sem, 16)
                        for name in ("Wo", "Wfv"):
                            for k in range(2):
                                ts(w(name, k), w(name, k), 0.5, None, ALU.mult).then_inc(folded.sem, 1)
                        ve.wait_ge(folded.sem, FOLDS)
                elif piece == "o":
                    ve.wait_ge(xa_in.sem, count(xa_in, g, 16))
                    ve.wait_ge(*a_ready(g, "o"))
                    for m in range(HALVES):
                        last = stt(y[:, m, :], a_bank("o")[:, m * T:(m + 1) * T], o_bias[:, m:m + 1], xa_sb[:, m, :], ALU.add, ALU.add)
                    last.then_inc(a_read("o"), 1)
                elif piece == "rms":
                    ve.wait_ge(ysq_made.sem, count(ysq_made, g, 1))
                    tt(ysum[:, :], ysq[:, 0, :], ysq[:, 1, :], ALU.add).then_inc(ysum_made.sem, 1)
                elif piece == "rrms":
                    ve.wait_ge(*a_taken(g, "rms"))
                    invert(a_ms[:, :], a_ms[:, :]).then_inc(arstd_made.sem, 1)
                elif piece == "yn":
                    ve.wait_ge(*a_ready(g, "rrms"))
                    tt(y[:, :, :], y[:, :, :], both(a_bank("rrms")[:, 0:T]), ALU.mult).then_inc(a_read("rrms"), 1)
                elif piece == "x1":
                    ve.wait_ge(*r_taken(g - 1, "O"))
                    ve.wait_ge(o_full.sem, count(o_full, g, BPS + 1))
                    for m in range(HALVES):
                        last = stt(x1[:, m, :], o_ps[:, m * T:(m + 1) * T], v("b2", m), xa_sb[:, m, :], ALU.add, ALU.add)
                    last.then_inc(o_free.sem, 1)

            def recurrent(g, piece):
                if piece in ("mean0", "mean1"):
                    n = int(piece[-1])
                    if n == 0:
                        ve.wait_ge(o_free.sem, count(o_free, g, BPS + 1))
                    else:
                        ve.wait_ge(*r_taken(g, "O"))
                    tt(hsum[n][:, :], (x1, x2)[n][:, 0, :], (x1, x2)[n][:, 1, :], ALU.add).then_inc(hsum_made[n].sem, 1)
                elif piece in ("cent0", "cent1"):
                    n = int(piece[-1])
                    ve.wait_ge(*r_ready(g, "mean", n))
                    tt(xc[n][:, :, :], (x1, x2)[n][:, :, :], both(r_bank("mean", n)[:, 0:T]), ALU.subtract).then_inc(r_read("mean", n), 1)
                elif piece in ("var0", "var1"):
                    n = int(piece[-1])
                    ve.wait_ge(sq_made[n].sem, count(sq_made[n], g, 1))
                    tt(hsum[n][:, :], sq[n][:, 0, :], sq[n][:, 1, :], ALU.add).then_inc(hsum_made[n].sem, 1)
                elif piece in ("rstd0", "rstd1"):
                    n = int(piece[-1])
                    ve.wait_ge(*r_taken(g, "var", n))
                    invert(r_ms[n][:, :], r_ms[n][:, :]).then_inc(rstd_made[n].sem, 1)
                elif piece in ("norm0", "norm1"):
                    n = int(piece[-1])
                    ve.wait_ge(*r_ready(g, "rstd", n))
                    tt(xc[n][:, :, :], xc[n][:, :, :], both(r_bank("rstd", n)[:, 0:T]), ALU.mult).then_inc(r_read("rstd", n), 1)
                elif piece in ("shift0", "shift1"):
                    n = int(piece[-1])
                    ve.wait_ge(*r_taken(g, "rstd", n))
                    name = ("ln1", "ln2")[n]
                    for h in range(HALVES):
                        last = ts(xs[n][:, h, :, 1:S + 1], by_batch(xc[n][:, h, :]), v(name + "_w", h), v(name + "_b", h), ALU.mult, ALU.add)
                    last.then_inc(xs_made[n].sem, 1)
                    ve.wait_ge(xs_made[n].sem, count(xs_made[n], g, 1))
                    ve.wait_ge(row_made[n].sem, count(row_made[n], g, 1))
                    rows = xs[n][:, :, :, :].rearrange("p h b s -> p (h b) s")
                    tt(batches(flat(sx[n])), rows[:, :, 0:S], rows[:, :, 1:S + 1], ALU.subtract).then_inc(sx_made[n].sem, 1)
                    ve.wait_ge(sx_made[n].sem, count(sx_made[n], g, 1))
                    if n == 0:
                        shift(z, 0, "maa_x", z_made)
                    else:
                        shift(xf[:, 0, :, :], 1, "fk", shift_made)
                        shift(xf[:, 1, :, :], 1, "fr", shift_made)
                elif piece[0] == "x":
                    n = int(piece[1])
                    ve.wait_ge(*r_ready(g, "x", n))
                    ve.wait_ge(xm_made.sem, count(xm_made, g, max(0, n - 1)))
                    for h in range(HALVES):
                        last = stt(tmp[:, n % 2, h, :], r_bank("x", n)[:, h * T:(h + 1) * T], v("maa", 2 * ORDER[n] + h), sx[0][:, h, :], ALU.add, ALU.mult)
                    last.then_inc(r_read("x", n), 1)
                elif piece == "gate":
                    ve.wait_ge(gt_made.sem, count(gt_made, g, 1))
                    stt(flat(gate), flat(gt), 1.0, r_bank("G")[:, :], ALU.add, ALU.mult).then_inc(r_read("G"), 1)
                    ve.wait_ge(*r_taken(g, "G"))
                    for h in range(HALVES):
                        last = ts(gt[:, h, :], gate[:, h, :], v("gn_b", h), None, ALU.mult)
                    last.then_inc(gate_b_made.sem, 1)
                    for h in range(HALVES):
                        last = ts(gate[:, h, :], gate[:, h, :], v("gn_w", h), None, ALU.mult)
                    last.then_inc(gate_made.sem, 1)
                elif piece[0] == "s" and piece[1].isdigit():
                    j = int(piece[1])
                    if j == 0:
                        ve.wait_ge(*r_taken(g, "K"))
                        ve.wait_ge(decay_made.sem, count(decay_made, g, 1))
                        ve.wait_ge(first_made.sem, count(first_made, g, 1))
                    ve.wait_ge(vb_in[j].sem, count(vb_in[j], g, 16))
                    tt(kv[:, j, :, 1:S], batches(vb[:, j, :])[:, :, 0:S - 1], batches(flat(kk))[:, :, 0:S - 1],
                       ALU.mult).then_inc(kv_made.sem, 1)
                    ve.wait_ge(kv_made.sem, count(kv_made, g, j + 1))
                    ve.wait_ge(rs_made.sem, count(rs_made, g, max(0, j - 1)))
                    nc.vector.tensor_tensor_scan(st[:, j % 2, :], decay[:, :, :, :].rearrange("p h b s -> p (h b s)"),
                                                 kv[:, j, :, :].rearrange("p b s -> p (b s)"), 0.0, ALU.mult, ALU.add).then_inc(st_made.sem, 1)
                elif piece == "coef":
                    ve.wait_ge(*r_ready(g, "coef"))
                    tt(flat(bonus), r_bank("coef")[:, :], flat(vr), ALU.mult).then_inc(r_read("coef"), 1)
                elif piece == "gn":
                    ve.wait_ge(gate_made.sem, count(gate_made, g, 1))
                    ve.wait_ge(gsq_made.sem, count(gsq_made, g, 1))
                    tt(flat(og), red_ps[:, :], flat(gate), ALU.mult).then_inc(gated.sem, 1)
                elif piece == "grstd":
                    ve.wait_ge(*r_taken(g, "gvar"))
                    invert(g_ms, g_ms).then_inc(grstd_made.sem, 1)
                elif piece == "gnorm":
                    ve.wait_ge(*r_ready(g, "grstd"))
                    tt(flat(og), flat(og), r_bank("grstd")[:, :], ALU.mult).then_inc(r_read("grstd"), 1)
                    ve.wait_ge(*r_taken(g, "grstd"))
                    tt(flat(og), flat(og), flat(gt), ALU.add).then_inc(og_made.sem, 1)
                elif piece == "res":
                    ve.wait_ge(out_done.sem, count(out_done, g, 0))
                    ve.wait_ge(*r_ready(g, "O"))
                    tt(flat(x2), r_bank("O")[:, :], flat(x1), ALU.add).then_inc(r_read("O"), 1)
                elif piece == "fin":
                    ve.wait_ge(*r_ready(g, "fv"))
                    ve.wait_ge(*r_taken(g, "fr"))
                    stt(flat(ft), flat(tr), 1.0, r_bank("fv")[:, :], ALU.add, ALU.mult).then_inc(r_read("fv"), 1)

            run(ve, attention, recurrent)

        @block.gpsimd
        def _(po):
            tt = nc.gpsimd.tensor_tensor
            po.memset(ones_bf[:, :], 1.0).then_inc(fills.sem, 1)
            po.memset(th[:, 1, :], 0.0).then_inc(fills.sem, 1)
            po.memset(tw[:, :], 0.0).then_inc(fills.sem, 1)
            po.memset(decay[:, :, :, 0], 0.0).then_inc(fills.sem, 1)
            po.wait_ge(fills.sem, FILLS)

            def attention(g, piece):
                if piece[0:2] == "in":
                    u = int(piece[2:])
                    po.wait_ge(rsum_made.sem, count(rsum_made, g, u + 1))
                    tt(probs[:, PROBS(u), :, :], probs[:, PROBS(u), :, :], rsum[:, u % 2, :].unsqueeze(2).broadcast_to([P, 4, KEYS]),
                       ALU.mult).then_inc(norm_made.sem, 1)

            def recurrent(g, piece):
                if piece[0] == "x":
                    n = int(piece[1])
                    po.wait_ge(*r_taken(g, "x", n))
                    tt(xm[:, n % 2, :, :].rearrange("p h (b s) -> p (h b) s", b=GB), tmp[:, n % 2, :, :].rearrange("p h (b s) -> p (h b) s", b=GB),
                       xs[0][:, :, :, :].rearrange("p h b s -> p (h b) s")[:, :, 1:S + 1], ALU.add).then_inc(xm_made.sem, 1)
                elif piece == "rk":
                    po.wait_ge(*r_taken(g, "R"))
                    tt(flat(rk), flat(rr), flat(kk), ALU.mult).then_inc(rk_made.sem, 1)
                elif piece[0] == "s" and piece[1].isdigit():
                    j = int(piece[1])
                    po.wait_ge(st_made.sem, count(st_made, g, j + 1))
                    po.wait_ge(gathered.sem, count(gathered, g, max(0, j - 3)))
                    tt(rs[:, j % 4, :], st[:, j % 2, :], flat(rr), ALU.mult).then_inc(rs_made.sem, 1)
                elif piece == "fk":
                    po.wait_ge(*r_taken(g, "fk"))
                    tt(flat(act), flat(relu), flat(relu), ALU.mult).then_inc(act_made.sem, 1)
                elif piece == "fin":
                    po.wait_ge(*r_taken(g, "fv"))
                    tt(flat(x2), flat(x2), flat(ft), ALU.add).then_inc(fin_made.sem, 1)

            run(po, attention, recurrent)


FILLS, FOLDS = 4, 11
BPS = GB // 2


def PROBS(u):
    return u % 3


def unit(u):
    return u // PAIRS, u % PAIRS


def kernel(**inputs):
    import numpy as np
    import concourse.bacc as bacc
    from concourse import mybir as my
    from concourse.bass_utils import run_bass_kernel_spmd

    a = {n: np.asarray(x) for n, x in inputs.items()}
    l0 = {n[len("L0_xattn_"):]: x for n, x in a.items() if n.startswith("L0_xattn_")}
    l1 = {n[len("L1_xattn_"):]: x for n, x in a.items() if n.startswith("L1_xattn_")}
    x, ctx = a["x"], a["ctx_2048"]

    def halves(m):
        return m.reshape(HALVES, P, -1).transpose(1, 0, 2)

    def grouped(z):
        return z.reshape(GROUPS, GB, z.shape[1], HALVES, P).transpose(0, 4, 3, 1, 2)

    kv_w = l0["kv_w"].reshape(C, C, 2)
    kv_b = l0["kv_b"].reshape(C, 2)
    weights = {"q": l0["q_w"], "k": kv_w[:, :, 0], "v": kv_w[:, :, 1], "o": l0["out_w"], "w1": l0["mlp_w1"],
               "maa1": l1["maa_w1"], "td1": l1["td_w1"], "Wr": l1["Wr"].T, "Wk": l1["Wk"].T, "Wv": l1["Wv"].T, "Wg": l1["Wg"].T,
               "Wo": l1["Wo"].T, "Wfk": l1["Wfk"].T, "Wfr": l1["Wfr"].T, "Wfv": l1["Wfv"].T}
    parity = (np.arange(P) // DH) % 2
    even, odd = (parity == 0).astype(np.float32), (parity == 1).astype(np.float32)
    vectors = {"q_b": l0["q_b"], "k_b": kv_b[:, 0], "v_b": kv_b[:, 1], "o_b": l0["out_b"], "pn": l0["postnorm_w"], "b1": l0["mlp_b1"],
               "b2": l0["mlp_b2"], "ln1_w": l1["ln1_w"], "ln1_b": l1["ln1_b"], "ln2_w": l1["ln2_w"], "ln2_b": l1["ln2_b"],
               "maa_x": l1["maa_x"], "maa": l1["maa_stack"].reshape(-1), "td": l1["time_decay"], "gn_w": l1["gn_w"], "gn_b": l1["gn_b"],
               "fk": l1["ffn_maa_k"], "fr": l1["ffn_maa_r"], "u": l1["u"].reshape(-1),
               "even": even, "odd": odd, "even16": even / np.float32(DH), "odd16": odd / np.float32(DH),
               "eps6": np.full(P, 1e-6, np.float32), "eps5": np.full(P, 1e-5, np.float32)}
    p = np.arange(P)
    same = (p[:, None] // RH == p[None, :] // RH).astype(np.float32)
    center = np.eye(P, dtype=np.float32) - same / np.float32(RH)
    by_head = np.zeros((P, P), np.float32)
    by_head[p, p // RH] = 1
    mats = {"ident": np.eye(P, dtype=np.float32), "mean256": np.full((P, P), 1 / C, np.float32), "mean8": by_head / np.float32(RH),
            "center8": center, "same_head": same}
    for c in range(QUARTERS):
        for n in (RH, C):
            mats[f"expand{n}_{c}"] = np.zeros((P, P), np.float32)
        mats[f"expand{RH}_{c}"][32 * c:32 * c + P // RH] = by_head.T[0:P // RH]
        mats[f"expand{C}_{c}"][32 * c] = 1
    for j in range(RH):
        mats[f"gather{j}"] = (same * ((p[None, :] % RH == j) - np.float32(1 / RH))).astype(np.float32)
    maa2 = np.zeros((P, MIX, C), np.float32)
    for f in range(MIX):
        row = DM * f % P
        maa2[row:row + DM, f, :] = l1["maa_w2"][f]
    td2 = np.zeros((P, C), np.float32)
    td2[0:DD] = l1["td_w2"]
    arrays = {
        "hT": grouped(np.concatenate([ctx, x], axis=1)),
        "xT": grouped(x).reshape(GROUPS, P, HALVES, T),
        "maskT": a["mask_BxS2_ik0"].reshape(GROUPS, T),
        "stT": grouped(ctx[:, 0:2]).transpose(0, 1, 4, 2, 3),
        "s0T": ctx[:, 2:2 + RH].reshape(GROUPS, GB, HALVES, P, RH).transpose(0, 3, 4, 2, 1),
        "W": np.concatenate([halves(weights[n]) for n in W_COLS], axis=2),
        "W2": l0["mlp_w2"].reshape(FM, P, C).transpose(1, 0, 2),
        "MAA2": maa2,
        "TD2": td2,
        "VEC": np.concatenate([vectors[n].reshape(-1, P).T for n in V_COLS], axis=1),
        "MATS": np.stack([mats[n] for n in M_NAMES], axis=1),
    }
    nc = bacc.Bacc("TRN2", target_bir_lowering=False, num_devices=1)
    arrays = {n: np.ascontiguousarray(z) for n, z in arrays.items()}
    args = {n: nc.dram_tensor(n, list(z.shape), my.dt.from_np(z.dtype), kind="ExternalInput").ap() for n, z in arrays.items()}
    out = nc.dram_tensor("out", [GROUPS, P, HALVES, T], my.dt.float32, kind="ExternalOutput").ap()
    build(nc, *[args[n] for n in ("hT", "xT", "maskT", "stT", "s0T", "W", "W2", "MAA2", "TD2", "VEC", "MATS")], out)
    r = run_bass_kernel_spmd(nc, [arrays], core_ids=[0])
    got = r.results[0]["out"]
    return got.reshape(GROUPS, P, HALVES, GB, S).transpose(0, 3, 4, 2, 1).reshape(B, S, C)
```
